# Optimizing a Trainium2 kernel written in Bass

```python
import numpy as np
import jax
import jax.numpy as jnp

def _softmax(x, axis=-1):
    return jax.nn.softmax(x, axis=axis)

def _gelu(x):
    return jax.nn.gelu(x, approximate=True)

def _silu(x):
    return jax.nn.silu(x)

def _sigmoid(x):
    return jax.nn.sigmoid(x)

def _layernorm(x, axis=-1, eps=1e-05):
    m = jnp.mean(x, axis=axis, keepdims=True)
    v = jnp.var(x, axis=axis, keepdims=True)
    return (x - m) / jnp.sqrt(v + eps)

def _scatter_add(tgt, idx, src, axis=0):
    return tgt.at[idx].add(src)

def _segment_sum(src, seg, n):
    return jax.ops.segment_sum(src, seg, n)
kernel_name = 'mk_adj_preln_d2_adj_r2_4a18cd'

def setup_inputs(seed: int=0):
    np.random.seed(seed)
    _w = jnp.asarray

    def _rec_inputs():
        import jax
        import jax.numpy as jnp
        _gk = jax.random.key(seed)
        x = -0.0005207 + 1.001 * jax.random.normal(jax.random.fold_in(_gk, 1), (2048, 256), jnp.float32)
        _w = (1.0 + jnp.arange(2048, dtype=jnp.float32)) ** (-0.5)
        _w = _w / _w.mean()
        _pij = jnp.clip(0.0078125 * _w[:, None] * _w[None, :], 0.0, 1.0)
        _a = jax.random.uniform(jax.random.fold_in(_gk, 2), (2048, 2048)) < _pij
        _af = _a.astype(jnp.float32)
        adj = _af
        return (x, adj)
    x, adj = _rec_inputs()

    def _L0_gnn_setup():
        import jax, jax.numpy as jnp
        import numpy as np
        N = 2048
        INPUT_DIM = 256
        KEY_DIM = 64
        OUT_DIM = 256
        N_HEADS = 8
        IDENTITY_BIAS = 0.01
        MASK_VAL = 1e+16

        def _xavier(key, shape, gain=np.sqrt(2.0)):
            std = gain * np.sqrt(2.0 / (shape[-2] + shape[-1]))
            return jax.random.normal(key, shape, dtype=jnp.float32) * np.float32(std)
        key = jax.random.key(seed)
        kx, ka, kk, kq, kv, ko = jax.random.split(key, 6)
        node_matrix = jax.random.normal(kx, (N, INPUT_DIM), dtype=jnp.float32)
        adjacency_matrix = jax.random.bernoulli(ka, 0.01, (N, N)).astype(jnp.float32)
        Wks = _xavier(kk, (N_HEADS, INPUT_DIM, KEY_DIM))
        Wqs = _xavier(kq, (N_HEADS, INPUT_DIM, KEY_DIM))
        Wvs = _xavier(kv, (N_HEADS, INPUT_DIM, KEY_DIM))
        Wo = _xavier(ko, (N_HEADS, KEY_DIM, OUT_DIM))
        return {'node_matrix': node_matrix, 'adjacency_matrix': adjacency_matrix, 'Wks': Wks, 'Wqs': Wqs, 'Wvs': Wvs, 'Wo': Wo}
    _L0_gnn_all = _L0_gnn_setup()
    _L0_gnn_in = {k: v for k, v in _L0_gnn_all.items() if k in ('Wks', 'Wqs', 'Wvs', 'Wo')}
    del _L0_gnn_all

    def _L1_gnn_setup():
        import jax, jax.numpy as jnp
        import numpy as np
        EPS = 1e-08
        key = jax.random.key(seed)
        k1, k2, k3, k4 = jax.random.split(key, 4)
        N, IN, OUT = (4096, 256, 256)
        x = jax.random.normal(k1, (N, IN), dtype=jnp.float32)
        adj = jax.random.uniform(k2, (N, N), dtype=jnp.float32)
        W = jax.random.normal(k3, (OUT, IN), dtype=jnp.float32) * (1.0 / np.sqrt(IN))
        b = jax.random.normal(k4, (OUT,), dtype=jnp.float32) * 0.01
        return {'x': x, 'adj': adj, 'W': W, 'b': b}
    _L1_gnn_all = _L1_gnn_setup()
    _L1_gnn_in = {k: v for k, v in _L1_gnn_all.items() if k in ('W', 'b')}
    del _L1_gnn_all
    return {'x': x, 'adj': adj, 'L0_gnn_Wks': _L0_gnn_in['Wks'], 'L0_gnn_Wqs': _L0_gnn_in['Wqs'], 'L0_gnn_Wvs': _L0_gnn_in['Wvs'], 'L0_gnn_Wo': _L0_gnn_in['Wo'], 'L1_gnn_W': _L1_gnn_in['W'], 'L1_gnn_b': _L1_gnn_in['b']}

def reference(x, adj, L0_gnn_Wks, L0_gnn_Wqs, L0_gnn_Wvs, L0_gnn_Wo, L1_gnn_W, L1_gnn_b):
    import jax
    import jax.numpy as jnp

    def _L0_gnn_ref(node_matrix, adjacency_matrix, Wks, Wqs, Wvs, Wo):
        import jax, jax.numpy as jnp
        import numpy as np
        N = 2048
        INPUT_DIM = 256
        KEY_DIM = 64
        OUT_DIM = 256
        N_HEADS = 8
        IDENTITY_BIAS = 0.01
        MASK_VAL = 1e+16

        def _xavier(key, shape, gain=np.sqrt(2.0)):
            std = gain * np.sqrt(2.0 / (shape[-2] + shape[-1]))
            return jax.random.normal(key, shape, dtype=jnp.float32) * np.float32(std)
        n = node_matrix.shape[0]
        kd = Wks.shape[-1]
        eye = jnp.eye(n, dtype=node_matrix.dtype)
        adj = jnp.maximum(adjacency_matrix, eye)
        q = jnp.einsum('nd,hdk->hnk', node_matrix, Wqs)
        k = jnp.einsum('nd,hdk->hnk', node_matrix, Wks)
        v = jnp.einsum('nd,hdk->hnk', node_matrix, Wvs)
        scores = jnp.einsum('hqk,hmk->hqm', q, k) * kd ** (-0.5)
        scores = scores + IDENTITY_BIAS * eye - MASK_VAL * (1.0 - adj)
        att = jax.nn.softmax(scores, axis=-1)
        return jnp.einsum('hqm,hmk,hko->qo', att, v, Wo)

    def _L1_gnn_ref(x, adj, W, b):
        import jax, jax.numpy as jnp
        import numpy as np
        EPS = 1e-08
        deg = adj.sum(axis=1)
        dis = (deg + EPS) ** (-0.5)
        a_norm = dis[:, None] * adj * dis[None, :]
        h = a_norm @ x
        return h @ W.T + b
    h = jnp.maximum(_layernorm(x, axis=-1), 0.0)
    x = x + _L0_gnn_ref(h, adj, L0_gnn_Wks, L0_gnn_Wqs, L0_gnn_Wvs, L0_gnn_Wo)
    h = jnp.maximum(_layernorm(x, axis=-1), 0.0)
    x = x + _L1_gnn_ref(h, adj, L1_gnn_W, L1_gnn_b)
    return x

_drawn_inputs = setup_inputs


def setup_inputs(seed=0):
    import zlib

    import numpy as np

    out = dict(_drawn_inputs(seed))
    spreads = {}
    factors = {'L1_gnn_b': 8.0}
    for name, (base, spread) in spreads.items():
        noise = np.random.default_rng([zlib.crc32(name.encode()), seed]).standard_normal(out[name].shape)
        drawn = base * np.exp(spread * noise) if base else spread * noise
        out[name] = jnp.asarray(drawn.astype(out[name].dtype))
    for name, factor in factors.items():
        out[name] = (out[name] * factor).astype(out[name].dtype)
    return out
```

```python
import concourse.bass as bass
from concourse import mybir
from contextlib import ExitStack


def aux_jobs(blocks, tiles_per_block, halves):
    jobs = [("proj", 0), ("proj", 1), ("value", 0)]
    rows = []
    for a in range(blocks * tiles_per_block * halves):
        jobs.append(("max", a))
        if (a + 1) % (tiles_per_block * halves) == 0:
            rows.append((a + 2, (a + 1) // (tiles_per_block * halves) - 1))
        if rows and a == rows[0][0]:
            jobs.append(("crow", rows.pop(0)[1]))
    assert [b for _, b in rows] == [blocks - 1]
    return jobs


def adj_preln_kernel(nc, x, adj, Wks, Wqs, Wvs, Wo, W1, b1, out):
    fp32 = mybir.dt.float32
    fp16 = mybir.dt.float16
    bf16 = mybir.dt.bfloat16
    ALU = mybir.AluOpType
    ACT = mybir.ActivationFunctionType

    N, D = x.shape
    H, _, KD = Wqs.shape
    P = 128
    NT = N // P
    KT = D // P
    HK = H * KD
    CT = HK // P
    QB = 512
    NB = N // QB
    TB = QB // P
    MP = NT // 2
    ST = NB * MP
    HALF = 1024
    LN_EPS, DEG_EPS = 1e-5, 1e-8
    BIG = float(2 ** 53)
    MASK_STEP, DIAG_EPS = mask_constants()
    WS = 64.0
    VW = 2 * KD + 1

    JOBS = aux_jobs(NB, TB, N // HALF)
    NJ = len(JOBS) + 1
    POS = {job: i for i, job in enumerate(JOBS)}

    def job(h, kind, i):
        return h * NJ + (len(JOBS) if (kind, i) == ("crow", NB - 1) else POS[(kind, i)])

    at_step = [[] for _ in range(ST)]
    at_step[1].append(("crow", NB - 1))
    at_step[0 + 1].append(("proj", 0))
    at_step[2].append(("proj", 1))
    at_step[3].append(("value", 0))
    rest = JOBS[3:]
    first = 4
    for n, j in enumerate(rest):
        at_step[first + n * (ST - first) // len(rest)].append(j)

    def pool_step(s):
        return s % 4 == 3

    def lo_count(h, s):
        mine = sum(pool_step(k) for k in range(s + 1))
        total = sum(pool_step(k) for k in range(ST))
        return h * (ST - total) + (s + 1 - mine), h * total + mine

    adj_rows = adj.rearrange("(t p) m -> t p m", p=P)
    x_rows = x.rearrange("(t p) d -> p t d", p=P)
    out_rows = out.rearrange("(t p) d -> p t d", p=P)
    mask_dram = nc.dram_tensor("mask_rows", (NT, P, N), bf16, kind="Internal").ap()

    ctx = ExitStack()
    with ctx:
        def sb(name, shape, dt):
            return ctx.enter_context(nc.sbuf_tensor(name, shape, dt))

        def pb(name, shape, dt):
            return ctx.enter_context(nc.psum_tensor(name, shape, dt))

        def sem(name):
            return ctx.enter_context(nc.semaphore(name))

        mask_T = sb("mask_T", [P, NT, N], bf16)
        mask_row = sb("mask_row", [P, 2, N], bf16)
        packs = sb("packs", [P, 2, 4, N], fp16)
        split_hi = sb("split_hi", [P, HALF], fp16)
        split_lo = sb("split_lo", [P, HALF], fp16)
        values = sb("values", [P, 2, NT, VW], fp16)
        hT = sb("hT", [P, 2, KT, N], fp16)
        wqk = sb("wqk", [P, 2, KT, H, 2 * KD], fp16)
        wv = sb("wv", [P, 2, KT, HK], fp16)
        work = sb("work", [P, 4 * 1024], fp32)
        heads_out = sb("heads_out", [P, NT, HK], fp32)
        wo = sb("wo", [P, CT, D], fp32)
        w1T = sb("w1T", [P, KT, D], fp32)
        bias = sb("bias", [P, D], fp32)
        junk = sb("junk", [P, HALF], bf16)
        id32 = sb("id32", [P, P], fp32)
        id16 = sb("id16", [P, P], fp16)
        idb = sb("idb", [P, P], bf16)
        mask_id = sb("mask_id", [P, P], fp16)
        diag_floor = sb("diag_floor", [P, P], bf16)
        cmax = sb("cmax", [P, 2, NT, 2], fp32)
        c16 = sb("c16", [P, 2, NT], fp16)
        o_lo = sb("o_lo", [P, TB, KD], fp32)
        o_sum = sb("o_sum", [P, TB, KD], fp32)
        o_rec = sb("o_rec", [P, TB], fp32)
        stats = sb("stats", [P, NT, 6], fp32)
        mv = sb("mv", [P, NT, 2], fp32)
        ve = sb("ve", [P, NT], fp32)
        root = sb("root", [P, NT], fp32)
        rstd = sb("rstd", [P, NT], fp32)
        newton = sb("newton", [P, NT], fp32)
        shift = sb("shift", [P, NT], fp32)
        deg = sb("deg", [P, NT], fp32)
        deg_root = sb("deg_root", [P, NT], fp32)
        dis = sb("dis", [P, NT], fp32)
        adj_diag = sb("adj_diag", [P, NT], fp32)

        def kA(p): return packs[:, p, 0, :]
        def kB(p): return packs[:, p, 1, :]
        def qA(p): return packs[:, p, 2, :]
        def qB(p): return packs[:, p, 3, :]

        def prob(s): return work[:, 1024 * (s % 2):1024 * (s % 2) + 1024]
        def prob_hi(s): return work[:, 2048 + 512 * (s % 2):2560 + 512 * (s % 2)].bitcast(fp16)
        def prob_lo(s): return work[:, 3072 + 512 * (s % 2):3584 + 512 * (s % 2)].bitcast(fp16)

        x_in = work[:, :].rearrange("p (t d) -> p t d", d=D)
        early = mask_T[:, :, :].rearrange("p t q -> p (t q)").bitcast(fp32)
        h_in = early[:, 0:NT * D].rearrange("p (t d) -> p t d", d=D)
        o = NT * D
        wqk_in = early[:, o:o + KT * HK * 2].rearrange("p (t h c) -> p t h c", t=KT, h=H)
        o += KT * HK * 2
        wv_in = early[:, o:o + KT * HK].rearrange("p (t c) -> p t c", t=KT)
        o += KT * HK
        w1_in = early[:, o:o + KT * D].rearrange("p (t c) -> p t c", t=KT)
        NA = 3
        rows_in = heads_out[:, :, :].rearrange("p t c -> p (t c)")[:, 0:NA * N]\
            .rearrange("p (b m) -> p b m", b=NA)
        deg_junk = heads_out[:, :, :].rearrange("p t c -> p (t c)")[:, NA * N:NA * N + N // 2].bitcast(bf16)

        x2 = packs[:, 0, :, :].rearrange("p a n -> p (a n)").bitcast(fp32)\
            .rearrange("p (t d) -> p t d", d=D)
        g_split = hT[:, :, :, :].rearrange("p a b n -> p (a b n)")\
            .rearrange("p (t a d) -> p t a d", a=2, d=D)

        def ot_sb(t): return work[:, 2048 + 512 * (t % 2):2560 + 512 * (t % 2)]
        def g_f(g): return work[:, 1024 * (g % 2):1024 * (g % 2) + 1024]
        def agg_sb(b): return work[:, 1024 * (b % 2):1024 * (b % 2) + 1024]

        scores_ps = [pb(f"scores_ps{i}", [P, 2, QB], fp32) for i in range(2)]
        aux_ps = pb("aux_ps", [P, 2, QB], fp32)
        acc_ps = pb("acc_ps", [P, 2, QB], fp32)
        acc = acc_ps[:, :, :].rearrange("p b (j c) -> p (b j) c", c=QB // 2)
        aux_flat = aux_ps[:, :, :].rearrange("p b c -> p (b c)")

        def sc_flat(i): return scores_ps[i % 2][:, :, :].rearrange("p b c -> p (b c)")
        def sc_bf(i): return sc_flat(i).bitcast(bf16)

        x_loaded = sem("x_loaded")
        w_loaded = sem("w_loaded")
        late_loaded = sem("late_loaded")
        rows_loaded = [sem(f"rows_loaded{i}") for i in range(NA)]
        mask_loaded = [sem(f"mask_loaded{i}") for i in range(2)]
        mask_stored = [sem(f"mask_stored{i}") for i in range(2)]
        x_again = sem("x_again")
        out_stored = sem("out_stored")
        consts = sem("consts")
        order_dve = sem("order_dve")
        order_pool = sem("order_pool")
        order_act = sem("order_act")
        var_ready = sem("var_ready")
        root_ready = sem("root_ready")
        rstd_ready = sem("rstd_ready")
        norm_done = sem("norm_done")
        tr_done = sem("tr_done")
        tr_hi = sem("tr_hi")
        tr_used = sem("tr_used")
        w_split = sem("w_split")
        w1_tr = sem("w1_tr")
        w1_used = sem("w1_used")
        deg_done = sem("deg_done")
        mask_built = sem("mask_built")
        maskT_filled = sem("maskT_filled")
        maskT_used = sem("maskT_used")
        aux_ready = sem("aux_ready")
        aux_done = sem("aux_done")
        packs_ready = sem("packs_ready")
        c_ready = sem("c_ready")
        proj_begun = sem("proj_begun")
        max_begun = sem("max_begun")
        scores_ready = sem("scores_ready")
        exp_done = sem("exp_done")
        hi_done = sem("hi_done")
        lo_dve = sem("lo_dve")
        lo_pool = sem("lo_pool")
        pv_done = sem("pv_done")
        acc_used = sem("acc_used")
        heads_done = sem("heads_done")
        ot_filled = sem("ot_filled")
        ot_ready = sem("ot_ready")
        wo_done = sem("wo_done")
        x2_done = sem("x2_done")
        g_norm = sem("g_norm")
        g_hi = sem("g_hi")
        g_ready = sem("g_ready")
        adjT_ready = sem("adjT_ready")
        x2b_ready = sem("x2b_ready")
        agg_done = sem("agg_done")
        agg_ready = sem("agg_ready")
        y_done = sem("y_done")
        y_ready = sem("y_ready")

        block = ctx.enter_context(nc.Block())
        NC = 5
        CROW_LAST = NB - 1

        @block.sync
        def _(sp):
            sp.dma_start(x_in, x_rows).then_inc(x_loaded, 16)
            for t in range(KT):
                for src, c in ((Wqs, 0), (Wks, KD)):
                    sp.dma_start(wqk_in[:, t, :, c:c + KD],
                                 src[:, t * P:(t + 1) * P, :].rearrange("h p k -> p h k")).then_inc(w_loaded, 16)
                sp.dma_start(wv_in[:, t, :].rearrange("p (h k) -> p h k", h=H),
                             Wvs[:, t * P:(t + 1) * P, :].rearrange("h p k -> p h k")).then_inc(w_loaded, 16)
            sp.dma_start(w1_in, W1.rearrange("(t p) d -> p t d", p=P)).then_inc(w_loaded, 16)

            def store_mask(t):
                sp.wait_ge(mask_built, t + 1)
                sp.dma_start(mask_dram[t], mask_row[:, t % 2, :]).then_inc(mask_stored[t % 2], 16)

            for t in range(NT):
                if t >= NA:
                    sp.wait_ge(deg_done, t - NA + 1)
                    sp.wait_ge(mask_built, t - NA + 1)
                sp.dma_start(rows_in[:, t % NA, :], adj_rows[t]).then_inc(rows_loaded[t % NA], 16)
                if t >= 2:
                    store_mask(t - 2)
            store_mask(NT - 2)
            store_mask(NT - 1)
            sp.dma_start(wo[:, :, :], Wo.rearrange("h k d -> (h k) d").rearrange("(c p) d -> p c d", p=P))\
                .then_inc(late_loaded, 16)
            sp.dma_start(bias[:, :], b1.rearrange("(a d) -> a d", a=1).to_broadcast([P, D])).then_inc(late_loaded, 16)
            for i in range(2):
                sp.wait_ge(mask_stored[i], 16 * (NT // 2))
            sp.wait_ge(maskT_filled, NT)

            def mask_rows(h):
                for t in range(NT):
                    last = job(h, "max", 2 * t - 3) if t >= 2 else job(h - 1, "max", 2 * (NT + t) - 3)
                    sp.wait_ge(aux_done, last + 1)
                    sp.dma_start(mask_row[:, t % 2, :], mask_dram[t]).then_inc(mask_loaded[t % 2], 16)

            mask_rows(1)
            with sp.Fori(0, (H - 2) // 2) as i:
                mask_rows(2 * i + 2)
                mask_rows(2 * i + 3)
            sp.wait_ge(scores_ready, (H - 1) * ST)
            sp.wait_ge(packs_ready, 2 * H)
            sp.dma_start(x2, x_rows).then_inc(x_again, 16)
            for t in range(NT):
                sp.wait_ge(y_ready, t + 1)
                sp.dma_start(out_rows[:, t, :], x2[:, t, :]).then_inc(out_stored, 16)
            sp.wait_ge(out_stored, 16 * NT)

        @block.gpsimd
        def _(pool):
            g = nc.gpsimd
            g.memset(id32[:, :], 0.0).then_inc(order_pool, 1)
            g.memset(diag_floor[:, :], -BIG).then_inc(order_pool, 1)
            pool.wait_ge(order_pool, 2)
            g.affine_select(out=id32[:, :], in_=id32[:, :], compare_op=ALU.not_equal, fill=1.0,
                            base=0, pattern=[[-1, P]], channel_multiplier=1).then_inc(consts, 1)
            g.affine_select(out=diag_floor[:, :], in_=diag_floor[:, :], compare_op=ALU.not_equal,
                            fill=DIAG_EPS, base=0, pattern=[[-1, P]], channel_multiplier=1).then_inc(consts, 1)
            pool.wait_ge(consts, 2)
            g.tensor_copy(id16[:, :], id32[:, :]).then_inc(consts, 1)
            g.tensor_copy(idb[:, :], id32[:, :]).then_inc(consts, 1)
            g.tensor_scalar(mask_id[:, :], id32[:, :], MASK_STEP, None, ALU.mult).then_inc(consts, 1)

            def low_parts(h):
                for s in range(ST):
                    if pool_step(s):
                        pool.wait_ge(hi_done, h * ST + s + 1)
                        g.tensor_tensor(prob_lo(s), prob(s), prob_hi(s), ALU.subtract).then_inc(lo_pool, 1)

            low_parts(0)
            with pool.Fori(0, (H - 2) // 2) as i:
                low_parts(2 * i + 1)
                low_parts(2 * i + 2)
            low_parts(H - 1)
            pool.wait_ge(late_loaded, 32)
            for b in range(NB):
                pool.wait_ge(g_norm, b + 1)
                rows = x2[:, b * TB:(b + 1) * TB, :]
                g.tensor_tensor(rows, rows, bias[:, :].rearrange("p (o d) -> p o d", o=1).to_broadcast([P, TB, D]),
                                ALU.add).then_inc(x2b_ready, 1)

        @block.scalar
        def _(act):
            a = nc.scalar
            act.wait_ge(var_ready, 1)
            a.activation(root[:, :], ve[:, :], ACT.Sqrt).then_inc(root_ready, 1)
            act.wait_ge(rstd_ready, 1)
            for t in range(NT):
                last = a.activation(h_in[:, t, :], x_in[:, t, :], ACT.Relu,
                                    bias=shift[:, t:t + 1], scale=rstd[:, t:t + 1])
                if t % 8 == 7:
                    last.then_inc(norm_done, 1)
            for g in range(2 * KT):
                half, t = g // KT, g % KT
                act.wait_ge(tr_done, g + 1)
                a.activation(hT[:, 0, t, half * HALF:(half + 1) * HALF], sc_flat(g), ACT.Copy).then_inc(tr_hi, 1)
            act.wait_ge(w1_tr, 1)
            a.activation(w1T[:, :, :].rearrange("p a b -> p (a b)"), aux_flat[:, 0:KT * D], ACT.Copy)\
                .then_inc(w1_used, 1)
            for t in range(NT):
                act.wait_ge(rows_loaded[t % NA], 16 * (t // NA + 1))
                if t >= 1:
                    act.wait_ge(deg_done, t)
                a.activation(deg_junk, rows_in[:, t % NA, :], ACT.Copy, accum_out=deg[:, t:t + 1]).then_inc(deg_done, 1)
                act.wait_ge(maskT_filled, t + 1)
                a.activation(mask_T[:, :, t * P:(t + 1) * P], sc_bf(t).rearrange("p (m q) -> p m q", q=P),
                             ACT.Copy).then_inc(maskT_used, 1)

            def probabilities(h, first):
                for s in range(ST):
                    n = h * ST + s
                    act.wait_ge(scores_ready, n + 1)
                    if not first or s >= 2:
                        ps = s - 2 if s >= 2 else s - 2 + ST
                        dve_n, pool_n = lo_count(h if s >= 2 else h - 1, ps)
                        if pool_step(ps):
                            act.wait_ge(lo_pool, pool_n)
                        else:
                            act.wait_ge(lo_dve, dve_n)
                    a.activation(prob(s), sc_flat(s), ACT.Exp).then_inc(exp_done, 1)
                    if not first or s >= 2:
                        act.wait_ge(pv_done, n - 1)
                    act.wait_ge(exp_done, n + 1)
                    a.activation(prob_hi(s), prob(s), ACT.Copy).then_inc(hi_done, 1)

            probabilities(0, True)
            with act.Fori(0, (H - 2) // 2) as i:
                probabilities(2 * i + 1, False)
                probabilities(2 * i + 2, False)
            probabilities(H - 1, False)

            act.wait_ge(var_ready, 2)
            a.activation(deg_root[:, :], dis[:, :], ACT.Sqrt).then_inc(root_ready, 1)
            act.wait_ge(pv_done, H * ST)
            for t in range(NT):
                act.wait_ge(ot_filled, t + 1)
                if t >= 2:
                    act.wait_ge(wo_done, t - 1)
                a.activation(ot_sb(t), scores_ps[t % 2][:, 0, :], ACT.Copy).then_inc(ot_ready, 1)
                if t % TB == TB - 1:
                    b = t // TB
                    act.wait_ge(var_ready, 3 + b)
                    a.activation(root[:, b * TB:t + 1], ve[:, b * TB:t + 1], ACT.Sqrt).then_inc(root_ready, 1)
                if t % TB == 2 and t > TB or t == NT - 1:
                    for b in ([t // TB - 1] if t < NT - 1 else [NB - 1]):
                        act.wait_ge(rstd_ready, 2 + b)
                        if b >= 2:
                            act.wait_ge(g_ready, b - 1)
                        for u in range(TB):
                            k = b * TB + u
                            last = a.activation(g_f(b)[:, u * D:(u + 1) * D], x2[:, k, :], ACT.Relu,
                                                bias=shift[:, k:k + 1], scale=rstd[:, k:k + 1])
                        last.then_inc(g_norm, 1)
                        act.wait_ge(g_norm, b + 1)
                        a.activation(g_split[:, b * TB:(b + 1) * TB, 0, :],
                                     g_f(b).rearrange("p (t d) -> p t d", d=D), ACT.Copy).then_inc(g_hi, 1)
            for b in range(NB):
                act.wait_ge(agg_done, b + 1)
                if b < 2:
                    act.wait_ge(g_ready, NB)
                else:
                    act.wait_ge(y_done, TB * (b - 1))
                a.activation(agg_sb(b), sc_flat(b), ACT.Copy).then_inc(agg_ready, 1)

        @block.vector
        def _(dve):
            v = nc.vector
            chain = {"base": 0, "n": 0}

            def link(ins):
                chain["n"] += 1
                return ins.then_inc(order_dve, 1)

            def settle():
                dve.wait_ge(order_dve, chain["base"] + chain["n"])

            def newton_rsqrt(y, r, value, w):
                link(v.reciprocal(y, r))
                settle()
                link(v.tensor_tensor(w, y, y, ALU.mult))
                settle()
                link(v.tensor_tensor(w, w, value, ALU.mult))
                settle()
                link(v.tensor_scalar(w, w, -0.5, 1.5, ALU.mult, ALU.add))
                settle()
                link(v.tensor_tensor(y, y, w, ALU.mult))
                settle()

            for p in range(2):
                link(v.memset(packs[64:65, p, 1, :], -1.0))
                link(v.memset(values[:, p, :, 2 * KD:VW], 1.0))
            dve.wait_ge(x_loaded, 16)
            for t in range(NT):
                link(v.bn_stats(stats[:, t, :], x_in[:, t, :]))
            settle()
            for t in range(NT):
                link(v.bn_aggr(mv[:, t, :], stats[:, t, :]))
            settle()
            v.tensor_scalar(ve[:, :], mv[:, :, 1], LN_EPS, None, ALU.add).then_inc(var_ready, 1)
            dve.wait_ge(root_ready, 1)
            newton_rsqrt(rstd[:, :], root[:, :], ve[:, :], newton[:, :])
            v.scalar_tensor_tensor(out=shift[:, :], in0=mv[:, :, 0], scalar=-1.0, in1=rstd[:, :],
                                   op0=ALU.mult, op1=ALU.mult).then_inc(rstd_ready, 1)
            dve.wait_ge(w_loaded, 16 * (3 * KT + 1))
            for src, dst, q in ((wqk_in[:, :, :, 0:KD], wqk[:, :, :, :, 0:KD], True),
                                (wqk_in[:, :, :, KD:2 * KD], wqk[:, :, :, :, KD:2 * KD], False),
                                (wv_in, wv[:, :, :, :], False)):
                scale = WS * KD ** -0.5 if q else WS
                for t in range(KT):
                    link(v.tensor_scalar(dst[:, 0, t], src[:, t], scale, None, ALU.mult))
                    settle()
                    link(v.scalar_tensor_tensor(out=dst[:, 1, t], in0=src[:, t], scalar=scale, in1=dst[:, 0, t],
                                                op0=ALU.mult, op1=ALU.subtract))
            settle()
            dve.sem_inc(w_split, 1)
            for g in range(2 * KT):
                half, t = g // KT, g % KT
                cols = slice(half * HALF, (half + 1) * HALF)
                dve.wait_ge(tr_hi, g + 1)
                v.tensor_tensor(hT[:, 1, t, cols], sc_flat(g), hT[:, 0, t, cols], ALU.subtract).then_inc(tr_used, 1)

            def drain(h, kind, i, par, in_loop, masks_here=False):
                n = job(h, kind, i)
                if kind == "proj":
                    dve.wait_ge(aux_ready, n + 1)
                    link(v.tensor_scalar(split_hi[:, :], aux_flat, 1.0 / WS, None, ALU.mult))
                    settle()
                    ins = v.scalar_tensor_tensor(out=split_lo[:, :], in0=aux_flat, scalar=1.0 / WS,
                                                 in1=split_hi[:, :], op0=ALU.mult, op1=ALU.subtract)
                    ins.then_inc(aux_done, 1)
                    cols = slice(i * HALF, (i + 1) * HALF)
                    dve.wait_ge(aux_done, n + 1)
                    if in_loop and i == 0 and not (isinstance(h, int) and h == 1):
                        dve.wait_ge(scores_ready, (h - 1) * ST)
                    v.tensor_copy(kA(par)[0:64, cols], split_hi[64:128, :])
                    v.tensor_copy(kA(par)[64:128, cols], split_hi[64:128, :])
                    v.tensor_copy(qA(par)[0:64, cols], split_hi[0:64, :])
                    v.tensor_copy(qA(par)[64:128, cols], split_lo[0:64, :])
                    v.tensor_copy(qB(par)[0:64, cols], split_hi[0:64, :])
                    v.tensor_copy(kB(par)[0:64, cols], split_lo[64:128, :]).then_inc(packs_ready, 1)
                    dve.wait_ge(packs_ready, 2 * h + i + 1)
                elif kind == "value":
                    vals = values[:, par, :, :]
                    src = aux_flat.rearrange("p (m k) -> p m k", k=KD)
                    if in_loop and not (isinstance(h, int) and h == 1):
                        dve.wait_ge(pv_done, (h - 1) * ST)
                    dve.wait_ge(aux_ready, n + 1)
                    link(v.tensor_scalar(vals[:, :, KD:2 * KD], src, 1.0 / WS, None, ALU.mult))
                    settle()
                    v.scalar_tensor_tensor(out=vals[:, :, 0:KD], in0=src, scalar=1.0 / WS,
                                           in1=vals[:, :, KD:2 * KD], op0=ALU.mult, op1=ALU.subtract)\
                        .then_inc(aux_done, 1)
                elif kind == "max":
                    t, half = i // 2, i % 2
                    if not masks_here and half == 0:
                        dve.wait_ge(mask_loaded[t % 2], 16 * ((h - 1) * (NT // 2) + t // 2 + 1))
                    dve.wait_ge(aux_ready, n + 1)
                    if in_loop:
                        dve.sem_inc(max_begun, 1)
                    v.tensor_tensor_reduce(out=junk[:, :], in0=aux_flat,
                                           in1=mask_row[:, t % 2, half * HALF:(half + 1) * HALF],
                                           scale=1.0, scalar=-3e38, op0=ALU.add, op1=ALU.max,
                                           accum_out=cmax[:, par, t, half:half + 1]).then_inc(aux_done, 1)
                    if i % (2 * TB) == 2 * TB - 1:
                        b = i // (2 * TB)
                        dve.wait_ge(aux_done, n + 1)
                        v.tensor_tensor(c16[:, par, b * TB:(b + 1) * TB], cmax[:, par, b * TB:(b + 1) * TB, 0],
                                        cmax[:, par, b * TB:(b + 1) * TB, 1], ALU.max).then_inc(c_ready, 1)
                else:
                    dve.wait_ge(aux_ready, n + 1)
                    v.tensor_copy(qB(par)[64:65, i * QB:(i + 1) * QB], aux_ps[0:1, 0, :]).then_inc(aux_done, 1)

            for kind, i in JOBS[0:3]:
                drain(0, kind, i, 0, False)
            dve.wait_ge(consts, NC)

            def build_mask(t):
                diag = slice(t * P, (t + 1) * P)
                dve.wait_ge(rows_loaded[t % NA], 16 * (t // NA + 1))
                link(v.tensor_tensor_reduce(out=o_sum[:, 0:P // KD, :].rearrange("p t k -> p (t k)"), in0=rows_in[:, t % NA, diag], in1=id32[:, :],
                                            scale=1.0, scalar=0.0, op0=ALU.mult, op1=ALU.add,
                                            accum_out=adj_diag[:, t:t + 1]))
                if t >= 2:
                    dve.wait_ge(mask_stored[t % 2], 16 * (t // 2))
                    dve.wait_ge(maskT_filled, t - 1)
                    dve.wait_ge(aux_done, job(0, "max", 2 * t - 3) + 1)
                link(v.tensor_scalar(mask_row[:, t % 2, :], rows_in[:, t % NA, :], -1.0, BIG, ALU.add, ALU.mult))
                settle()
                v.tensor_tensor(mask_row[:, t % 2, diag], mask_row[:, t % 2, diag], diag_floor[:, :],
                                ALU.max).then_inc(mask_built, 1)

            queue = list(JOBS[3:])
            for t in range(NT + 1):
                if t < NT:
                    build_mask(t)
                while t >= 1 and queue and (queue[0][0] == "crow" or queue[0][1] < 2 * t):
                    kind, i = queue.pop(0)
                    if kind == "max" and i % 2 == 0:
                        dve.wait_ge(mask_built, i // 2 + 1)
                    drain(0, kind, i, 0, False, masks_here=True)

            def evacuate(h, b):
                settle()
                link(v.reciprocal(o_rec[:, :], acc[:, :, 2 * KD]))
                link(v.tensor_copy(o_lo[:, :, :], acc[:, :, 0:KD]))
                settle()
                v.tensor_tensor(o_sum[:, :, :], acc[:, :, KD:2 * KD], o_lo[:, :, :], ALU.add).then_inc(acc_used, 1)
                dve.wait_ge(acc_used, NB * h + b + 1)
                link(v.tensor_tensor(heads_out[:, b * TB:(b + 1) * TB, bass.ds(h * KD, KD)], o_sum[:, :, :],
                                     o_rec[:, :].rearrange("p (t o) -> p t o", o=1).to_broadcast([P, TB, KD]),
                                     ALU.mult))

            LINKS = 3 * NB + 3
            links0 = chain["n"]

            def period(h, par, first, last):
                if not first:
                    chain["base"], chain["n"] = LINKS * h + (links0 - 3), 0
                for s in range(ST):
                    if (s - 2) % MP == MP - 1 and (s >= 2):
                        dve.wait_ge(pv_done, h * ST + s - 1)
                        evacuate(h, (s - 2) // MP)
                    if s == 1 and not first:
                        dve.wait_ge(pv_done, h * ST)
                        evacuate(h - 1, NB - 1)
                    for kind, i in at_step[s]:
                        if (kind, i) == ("crow", CROW_LAST):
                            drain(h, kind, i, par, True)
                        elif not last:
                            drain(h + 1, kind, i, 1 - par, True)
                    if not pool_step(s):
                        dve.wait_ge(hi_done, h * ST + s + 1)
                        v.tensor_tensor(prob_lo(s), prob(s), prob_hi(s), ALU.subtract).then_inc(lo_dve, 1)
                if not last:
                    want = LINKS - (3 if first else 0)
                    assert chain["n"] - (links0 if first else 0) == want, (chain["n"], want)

            period(0, 0, True, False)
            with dve.Fori(0, (H - 2) // 2) as i:
                period(2 * i + 1, 1, False, False)
                period(2 * i + 2, 0, False, False)
            period(H - 1, 1, False, True)
            dve.wait_ge(pv_done, H * ST)
            evacuate(H - 1, NB - 1)
            settle()
            dve.sem_inc(heads_done, 1)

            link(v.tensor_scalar(adj_diag[:, :], adj_diag[:, :], -1.0, None, ALU.add))
            link(v.tensor_scalar(dis[:, :], deg[:, :], DEG_EPS, None, ALU.add))
            settle()
            dve.sem_inc(var_ready, 1)
            for t in range(NT):
                link(v.tensor_scalar(mask_T[:, t, :], mask_T[:, t, :], 1.0 / BIG, 1.0, ALU.mult, ALU.add))
            settle()
            for t in range(NT):
                blk = mask_T[:, t, t * P:(t + 1) * P]
                v.scalar_tensor_tensor(out=blk, in0=idb[:, :], scalar=adj_diag[:, t:t + 1], in1=blk,
                                       op0=ALU.mult, op1=ALU.add).then_inc(adjT_ready, 1)
            dve.wait_ge(root_ready, 2)
            link(v.tensor_copy(ve[:, :], dis[:, :]))
            settle()
            newton_rsqrt(dis[:, :], deg_root[:, :], ve[:, :], newton[:, :])
            dve.wait_ge(x_again, 16)
            for t in range(NT):
                dve.wait_ge(wo_done, t + 1)
                link(v.tensor_tensor(x2[:, t, :], x2[:, t, :], aux_ps[:, t % 2, 0:D], ALU.add))
                settle()
                dve.sem_inc(x2_done, 1)
                link(v.bn_stats(stats[:, t, :], x2[:, t, :]))
                settle()
                link(v.bn_aggr(mv[:, t, :], stats[:, t, :]))
                if t % TB == TB - 1:
                    b = t // TB
                    cols = slice(b * TB, t + 1)
                    settle()
                    link(v.tensor_scalar(ve[:, cols], mv[:, cols, 1], LN_EPS, None, ALU.add))
                    settle()
                    dve.sem_inc(var_ready, 1)
                    dve.wait_ge(root_ready, 3 + b)
                    newton_rsqrt(rstd[:, cols], root[:, cols], ve[:, cols], newton[:, cols])
                    link(v.scalar_tensor_tensor(out=rstd[:, cols], in0=rstd[:, cols], scalar=0.25, in1=dis[:, cols],
                                                op0=ALU.mult, op1=ALU.mult))
                    settle()
                    link(v.scalar_tensor_tensor(out=shift[:, cols], in0=mv[:, cols, 0], scalar=-1.0,
                                                in1=rstd[:, cols], op0=ALU.mult, op1=ALU.mult))
                    settle()
                    dve.sem_inc(rstd_ready, 1)
                if t % TB == TB - 1 and t >= 2 * TB - 1 or t == NT - 1:
                    for b in ([t // TB - 1] + ([NB - 1] if t == NT - 1 else [])):
                        dve.wait_ge(g_hi, b + 1)
                        v.tensor_tensor(g_split[:, b * TB:(b + 1) * TB, 1, :],
                                        g_f(b).rearrange("p (t d) -> p t d", d=D),
                                        g_split[:, b * TB:(b + 1) * TB, 0, :], ALU.subtract).then_inc(g_ready, 1)
            link(v.tensor_scalar(dis[:, :], dis[:, :], 4.0, None, ALU.mult))
            settle()
            dve.wait_ge(x2b_ready, NB)
            for t in range(NT):
                dve.wait_ge(y_done, t + 1)
                v.scalar_tensor_tensor(out=x2[:, t, :], in0=acc_ps[:, t % 2, 0:D], scalar=dis[:, t:t + 1],
                                       in1=x2[:, t, :], op0=ALU.mult, op1=ALU.add).then_inc(y_ready, 1)

        @block.tensor
        def _(pe):
            m = nc.tensor
            pe.wait_ge(consts, NC)
            for g in range(2 * KT):
                half, t = g // KT, g % KT
                if t == 0:
                    pe.wait_ge(norm_done, half + 1)
                if g >= 2:
                    pe.wait_ge(tr_used, g - 1)
                for u in range(8):
                    last = m.transpose(sc_flat(g)[:, u * P:(u + 1) * P], h_in[:, half * 8 + u, t * P:(t + 1) * P],
                                       id32[:, :])
                last.then_inc(tr_done, 1)
            pe.wait_ge(w_loaded, 16 * (3 * KT + 1))
            for t in range(KT):
                for u in range(KT):
                    last = m.transpose(aux_flat[:, t * D + u * P:t * D + (u + 1) * P],
                                       w1_in[:, u, t * P:(t + 1) * P], id32[:, :])
            last.then_inc(w1_tr, 1)
            pe.wait_ge(w1_used, 1)
            pe.wait_ge(w_split, 1)
            pe.wait_ge(tr_used, 2 * KT)

            TERMS = ((0, 0), (1, 0), (0, 1))

            def fill(h, kind, i, par, in_loop):
                n = job(h, kind, i)
                if kind == "max" and i == 0:
                    pe.wait_ge(packs_ready, 2 * h + 2)
                if kind == "crow":
                    pe.wait_ge(c_ready, NB * h + i + 1)
                if in_loop or n >= 1:
                    pe.wait_ge(aux_done, n)
                if kind == "proj":
                    if in_loop:
                        pe.sem_inc(proj_begun, 1)
                    for c in range(2):
                        cols = slice(i * HALF + c * QB, i * HALF + (c + 1) * QB)
                        steps = [(t, wp, hp) for t in range(KT) for wp, hp in TERMS]
                        for k, (t, wp, hp) in enumerate(steps):
                            weights = wqk[:, wp, t, :, :].rearrange("p h c -> p (h c)")
                            last = m.matmul(aux_ps[:, c, :], weights[:, bass.ds(h * 2 * KD, 2 * KD)],
                                            hT[:, hp, t, cols], start=(k == 0), stop=(k == len(steps) - 1))
                elif kind == "value":
                    for u in range(NT):
                        steps = [(t, wp, hp) for t in range(KT) for wp, hp in TERMS]
                        for k, (t, wp, hp) in enumerate(steps):
                            last = m.matmul(aux_flat[:, u * KD:(u + 1) * KD], hT[:, hp, t, u * P:(u + 1) * P],
                                            wv[:, wp, t, bass.ds(h * KD, KD)],
                                            start=(k == 0), stop=(k == len(steps) - 1))
                elif kind == "max":
                    t, half = i // 2, i % 2
                    for c in range(2):
                        k0 = half * HALF + c * QB
                        last = m.matmul(aux_ps[:, c, :], qA(par)[:, t * P:(t + 1) * P], kA(par)[:, k0:k0 + QB],
                                        start=True, stop=True)
                else:
                    for u in range(TB):
                        last = m.matmul(aux_ps[0:1, 0, u * P:(u + 1) * P], c16[:, par, i * TB + u:i * TB + u + 1],
                                        id16[:, :], start=True, stop=True)
                last.then_inc(aux_ready, 1)

            for kind, i in JOBS[0:3]:
                fill(0, kind, i, 0, False)
            queue = list(JOBS[3:])
            for t in range(NT + 1):
                if t < NT:
                    pe.wait_ge(mask_built, t + 1)
                    if t >= 2:
                        pe.wait_ge(maskT_used, t - 1)
                    for u in range(NT):
                        last = m.transpose(sc_bf(t)[:, u * P:(u + 1) * P], mask_row[:, t % 2, u * P:(u + 1) * P],
                                           idb[:, :])
                    last.then_inc(maskT_filled, 1)
                while t >= 1 and queue and (queue[0][0] == "crow" or queue[0][1] < 2 * t):
                    fill(0, *queue.pop(0), 0, False)
            pe.wait_ge(maskT_used, NT)

            def scores(h, s, par, first):
                b, pair = s // MP, s % MP
                if s % MP == 0:
                    pe.wait_ge(aux_done, job(h, "crow", b) + 1)
                if not first or s >= 2:
                    pe.wait_ge(exp_done, h * ST + s - 1)
                q = slice(b * QB, (b + 1) * QB)
                for a in range(2):
                    t = 2 * pair + a
                    k = slice(t * P, (t + 1) * P)
                    dst = scores_ps[s % 2][:, a, :]
                    m.matmul(dst, kA(par)[:, k], qA(par)[:, q], start=True, stop=False)
                    m.matmul(dst, kB(par)[0:65, k], qB(par)[0:65, q], start=False, stop=False)
                    last = m.matmul(dst, mask_id[:, :], mask_T[:, t, q], start=False, stop=True)
                last.then_inc(scores_ready, 1)

            def weigh(h, s, par, first):
                b, pair = s // MP, s % MP
                dve_n, pool_n = lo_count(h, s)
                if pool_step(s):
                    pe.wait_ge(lo_pool, pool_n)
                else:
                    pe.wait_ge(lo_dve, dve_n)
                if pair == 0 and not (first and b == 0):
                    pe.wait_ge(acc_used, NB * h + b)
                for a in range(2):
                    t = 2 * pair + a
                    for u in range(TB):
                        cols = slice(a * QB + u * P, a * QB + (u + 1) * P)
                        m.matmul(acc[:, u, 0:VW], prob_hi(s)[:, cols], values[:, par, t, :],
                                 start=(t == 0 and u % 2 == 0), stop=False, skip_group_check=True)
                        last = m.matmul(acc[:, u, KD:VW], prob_lo(s)[:, cols], values[:, par, t, KD:VW],
                                        start=False, stop=(t == NT - 1), skip_group_check=True)
                last.then_inc(pv_done, 1)

            def period(h, par, first, last):
                for s in range(ST):
                    scores(h, s, par, first)
                    if s >= 2:
                        weigh(h, s - 2, par, first)
                    elif not first:
                        weigh(h - 1, ST + s - 2, 1 - par, False)
                    for kind, i in at_step[s]:
                        if (kind, i) == ("crow", CROW_LAST):
                            fill(h, kind, i, par, True)
                        elif not last:
                            fill(h + 1, kind, i, 1 - par, True)

            period(0, 0, True, False)
            with pe.Fori(0, (H - 2) // 2) as i:
                period(2 * i + 1, 1, False, False)
                period(2 * i + 2, 0, False, False)
            period(H - 1, 1, False, True)
            weigh(H - 1, ST - 2, 1, False)
            weigh(H - 1, ST - 1, 1, False)

            pe.wait_ge(heads_done, 1)
            pe.wait_ge(late_loaded, 32)
            for t in range(NT + 1):
                if t < NT:
                    if t >= 2:
                        pe.wait_ge(ot_ready, t - 1)
                    for c in range(CT):
                        last = m.transpose(scores_ps[t % 2][:, 0, c * P:(c + 1) * P],
                                           heads_out[:, t, c * P:(c + 1) * P], id32[:, :])
                    last.then_inc(ot_filled, 1)
                if t >= 1:
                    k = t - 1
                    pe.wait_ge(ot_ready, k + 1)
                    if k >= 2:
                        pe.wait_ge(x2_done, k - 1)
                    for c in range(CT):
                        last = m.matmul(aux_ps[:, k % 2, 0:D], ot_sb(k)[:, c * P:(c + 1) * P], wo[:, c, :],
                                        start=(c == 0), stop=(c == CT - 1))
                    last.then_inc(wo_done, 1)

            pe.wait_ge(adjT_ready, NT)
            pe.wait_ge(g_ready, NB)

            def aggregate(b):
                if b >= 2:
                    pe.wait_ge(agg_ready, b - 1)
                for c in range(KT):
                    for t in range(NT):
                        for part in range(2):
                            last = m.matmul(scores_ps[b % 2][:, c, :], g_split[:, t, part, c * P:(c + 1) * P],
                                            mask_T[:, t, b * QB:(b + 1) * QB],
                                            start=(t == 0 and part == 0), stop=(t == NT - 1 and part == 1))
                last.then_inc(agg_done, 1)

            def transform(b):
                pe.wait_ge(agg_ready, b + 1)
                for u in range(TB):
                    t = b * TB + u
                    if t >= 2:
                        pe.wait_ge(y_ready, t - 1)
                    for c in range(KT):
                        last = m.matmul(acc_ps[:, t % 2, 0:D],
                                        agg_sb(b)[:, c * QB + u * P:c * QB + (u + 1) * P],
                                        w1T[:, c, :], start=(c == 0), stop=(c == KT - 1))
                    last.then_inc(y_done, 1)

            aggregate(0)
            for b in range(1, NB):
                aggregate(b)
                transform(b - 1)
            transform(NB - 1)


def mask_constants():
    best = None
    for i in range(1024):
        step = 1 + i / 1024
        want = 0.01 / step
        unit = 2.0 ** (-7 - 7)
        if want < 2.0 ** -7:
            unit /= 2
        eps = round(want / unit) * unit
        miss = abs(step * eps - 0.01)
        if best is None or miss < best[0]:
            best = (miss, step, eps)
    assert best[0] < 2e-8
    return best[1], best[2]


_INS = ['x', 'adj', 'L0_gnn_Wks', 'L0_gnn_Wqs', 'L0_gnn_Wvs', 'L0_gnn_Wo', 'L1_gnn_W', 'L1_gnn_b']
_OUTS = [((2048, 256), 'float32')]


def kernel(**inputs):
    import numpy as _np
    import concourse.bacc as _bacc
    from concourse import mybir as _mybir
    from concourse.bass_utils import run_bass_kernel_spmd as _run

    nc = _bacc.Bacc("TRN2", target_bir_lowering=False, num_devices=1)
    arrays, args = {}, []
    for name in _INS:
        a = _np.ascontiguousarray(inputs[name])
        arrays[f"in_{name}_dram"] = a
        args.append(nc.dram_tensor(f"in_{name}_dram", a.shape, _mybir.dt.from_np(a.dtype), kind="ExternalInput").ap())
    for i, (shape, dtype) in enumerate(_OUTS):
        dt = _mybir.dt.from_np(_np.dtype(dtype))
        args.append(nc.dram_tensor(f"out_{i}_dram", shape, dt, kind="ExternalOutput").ap())
    adj_preln_kernel(nc, *args)
    r = _run(nc, [arrays], core_ids=[0])
    got = tuple(r.results[0][f"out_{i}_dram"] for i in range(len(_OUTS)))
    return got[0]
```

```python
import concourse.bass as bass
from concourse import mybir
from contextlib import ExitStack


LAG = 3
LAG_BUFS = 4
LEAD = 3
PIECES = (1.3, 1.3, 0.65, 0.65)
AHEAD = (1.3, 7.8, 14.3, 20.8)
SPACING = 0.99


def place_jobs(jobs, steps):
    places, at = [], 0.0
    for _ in range(steps):
        for piece in PIECES:
            at += piece
            places.append(at)
    rest = (at - AHEAD[-1] - 3.0) / (len(jobs) - len(AHEAD)) * SPACING
    out, p = [[] for _ in places], 0
    for n, job in enumerate(jobs):
        want = AHEAD[n] if n < len(AHEAD) else AHEAD[-1] + 3.0 + (n - len(AHEAD)) * rest
        while places[p] < want - 1e-6:
            p += 1
        out[p].append(job)
    return out


def aux_jobs(blocks, tiles_per_block, halves):
    jobs = [("proj", 0), ("proj", 1), ("value", 0)]
    rows = []
    for a in range(blocks * tiles_per_block * halves):
        jobs.append(("max", a))
        if (a + 1) % (2 * tiles_per_block * halves) == 0:
            rows.append((a + 2, (a + 1) // (2 * tiles_per_block * halves) - 1))
        if rows and a == rows[0][0]:
            jobs.append(("crow", rows.pop(0)[1]))
    assert [b for _, b in rows] == [blocks // 2 - 1]
    return jobs


def adj_preln_kernel(nc, x, adj, Wks, Wqs, Wvs, Wo, W1, b1, out):
    fp32 = mybir.dt.float32
    fp16 = mybir.dt.float16
    bf16 = mybir.dt.bfloat16
    ALU = mybir.AluOpType
    ACT = mybir.ActivationFunctionType

    N, D = x.shape
    H, _, KD = Wqs.shape
    P = 128
    NT = N // P
    KT = D // P
    HK = H * KD
    CT = HK // P
    QB = 512
    NB = N // QB
    TB = QB // P
    MP = NT // 2
    ST = NB * MP
    HALF = 1024
    LN_EPS, DEG_EPS = 1e-5, 1e-8
    BIG = float(2 ** 53)
    MASK_STEP, DIAG_EPS = mask_constants()
    WS = 64.0
    VW = 2 * KD + 1

    JOBS = aux_jobs(NB, TB, N // HALF)
    NJ = len(JOBS) + 1
    POS = {job: i for i, job in enumerate(JOBS)}
    CROW_LAST = ("crow", NB // 2 - 1)
    PERIOD = JOBS[:LEAD] + [CROW_LAST] + JOBS[LEAD:]

    def job(h, kind, i):
        if (kind, i) == CROW_LAST:
            return (h + 1) * NJ + (LEAD - 1 if not (isinstance(h, int) and h == H - 1) else -1)
        n = POS[(kind, i)]
        if isinstance(h, int) and h == 0:
            return n
        return h * NJ + n - (n < LEAD)

    at_slot = place_jobs(PERIOD, ST)

    def head0_jobs(t):
        first = 0 if t == 3 else 2 * (t - 1)
        jobs = [n for n, (kind, i) in enumerate(JOBS) if kind == "max" and first <= i < 2 * t]
        lo, hi = jobs[0], jobs[-1] + 1
        if JOBS[lo - 1][0] == "crow" and lo > 0:
            lo -= 1
        if JOBS[hi - 1:hi] and t == NT:
            hi = len(JOBS)
        mine = JOBS[lo:hi]
        cut = max(1, len(mine) - 1)
        return mine[:cut], mine[cut:]

    def pool_step(s):
        return s % 2 == 1

    def lo_count(h, s):
        mine = sum(pool_step(k) for k in range(s + 1))
        total = sum(pool_step(k) for k in range(ST))
        return h * (ST - total) + (s + 1 - mine), h * total + mine

    adj_rows = adj.rearrange("(t p) m -> t p m", p=P)
    x_rows = x.rearrange("(t p) d -> p t d", p=P)
    out_rows = out.rearrange("(t p) d -> p t d", p=P)
    mask_dram = nc.dram_tensor("mask_rows", (NT, P, N), bf16, kind="Internal").ap()

    ctx = ExitStack()
    with ctx:
        def sb(name, shape, dt):
            return ctx.enter_context(nc.sbuf_tensor(name, shape, dt))

        def pb(name, shape, dt):
            return ctx.enter_context(nc.psum_tensor(name, shape, dt))

        def sem(name):
            return ctx.enter_context(nc.semaphore(name))

        mask_T = sb("mask_T", [P, NT, N], bf16)
        mask_row = sb("mask_row", [P, 2, N], bf16)
        packs = sb("packs", [P, 2, 4, N], fp16)
        split_hi = sb("split_hi", [P, HALF], fp16)
        split_lo = sb("split_lo", [P, HALF], fp16)
        values = sb("values", [P, 2, NT, VW], fp16)
        hT = sb("hT", [P, 2, KT, N], fp16)
        wqk = sb("wqk", [P, 2, KT, H, 2 * KD], fp16)
        wv = sb("wv", [P, 2, KT, HK], fp16)
        work = sb("work", [P, 6 * 1024], fp32)
        heads_out = sb("heads_out", [P, NT, HK], fp32)
        junk = sb("junk", [P, HALF], bf16)
        id32 = sb("id32", [P, P], fp32)
        id16 = sb("id16", [P, P], fp16)
        idb = sb("idb", [P, P], bf16)
        mask_id = sb("mask_id", [P, P], fp16)
        diag_floor = sb("diag_floor", [P, P], bf16)
        cmax = sb("cmax", [P, 2, NT, N // QB], fp32)
        c16 = sb("c16", [P, 2, NT], fp16)
        o_lo = sb("o_lo", [P, TB, KD], fp32)
        o_sum = sb("o_sum", [P, TB, KD], fp32)
        o_rec = sb("o_rec", [P, TB], fp32)
        stats = sb("stats", [P, NT, 6], fp32)
        mv = sb("mv", [P, NT, 2], fp32)
        ve = sb("ve", [P, NT], fp32)
        root = sb("root", [P, NT], fp32)
        rstd = sb("rstd", [P, NT], fp32)
        newton = sb("newton", [P, NT], fp32)
        shift = sb("shift", [P, NT], fp32)
        deg = sb("deg", [P, NT], fp32)
        deg_root = sb("deg_root", [P, NT], fp32)
        dis = sb("dis", [P, NT], fp32)
        adj_diag = sb("adj_diag", [P, NT], fp32)

        def kA(p): return packs[:, p, 0, :]
        def kB(p): return packs[:, p, 1, :]
        def qA(p): return packs[:, p, 2, :]
        def qB(p): return packs[:, p, 3, :]

        def prob(s): return work[:, 1024 * (s % 2):1024 * (s % 2) + 1024]
        def prob_hi(s): return work[:, 2048 + 512 * (s % LAG_BUFS):2560 + 512 * (s % LAG_BUFS)].bitcast(fp16)
        def prob_lo(s): return work[:, 4096 + 512 * (s % LAG_BUFS):4608 + 512 * (s % LAG_BUFS)].bitcast(fp16)

        x_in = work[:, 0:NT * D].rearrange("p (t d) -> p t d", d=D)
        h_in = x_in
        wqk_in = work[:, NT * D:NT * D + KT * HK * 2].rearrange("p (t h c) -> p t h c", t=KT, h=H)
        NA = 3
        heads_flat = heads_out[:, :, :].rearrange("p t c -> p (t c)")
        rows_in = heads_flat[:, 0:NA * N].rearrange("p (b m) -> p b m", b=NA)
        wv_in = heads_flat[:, NA * N:NA * N + KT * HK].rearrange("p (t c) -> p t c", t=KT)
        NM = 6
        mask_packs = packs[:, 1, :, :].bitcast(bf16)

        def mask_buf(t):
            return mask_packs[:, t % NM, :] if t % NM < 4 else mask_row[:, t % NM - 4, :]

        def masks_stored(eng):
            for i in range(NM):
                eng.wait_ge(mask_stored[i], 16 * len(range(i, NT, NM)))

        late = wqk[:, :, :, :, :].rearrange("p a t h c -> p (a t h c)").bitcast(fp32)
        wo = late[:, 0:CT * D].rearrange("p (c d) -> p c d", d=D)
        w1_in = late[:, CT * D:(CT + KT) * D].rearrange("p (t d) -> p t d", d=D)
        bias = late[:, (CT + KT) * D:(CT + KT + 1) * D]
        w1T = wv[:, :, :, :].rearrange("p a t c -> p (a t c)").bitcast(fp32)[:, 0:KT * D]\
            .rearrange("p (t d) -> p t d", d=D)

        x2 = packs[:, 0, :, :].rearrange("p a n -> p (a n)").bitcast(fp32)\
            .rearrange("p (t d) -> p t d", d=D)
        g_split = hT[:, :, :, :].rearrange("p a b n -> p (a b n)")\
            .rearrange("p (t a d) -> p t a d", a=2, d=D)

        def ot_sb(t): return work[:, 2048 + 512 * (t % 2):2560 + 512 * (t % 2)]
        def g_f(g): return work[:, 1024 * (g % 2):1024 * (g % 2) + 1024]
        def agg_sb(b): return work[:, 1024 * (b % 2):1024 * (b % 2) + 1024]

        scores_ps = [pb(f"scores_ps{i}", [P, 2, QB], fp32) for i in range(2)]
        aux_ps = pb("aux_ps", [P, 2, QB], fp32)
        acc_ps = pb("acc_ps", [P, 2, QB], fp32)
        acc = acc_ps[:, :, :].rearrange("p b (j c) -> p (b j) c", c=QB // 2)
        aux_flat = aux_ps[:, :, :].rearrange("p b c -> p (b c)")

        def sc_flat(i): return scores_ps[i % 2][:, :, :].rearrange("p b c -> p (b c)")
        def group_ps(g):
            return (sc_flat(0), sc_flat(1), aux_flat, acc_ps[:, :, :].rearrange("p b c -> p (b c)"))[g]
        def sc_bf(i): return sc_flat(i).bitcast(bf16)

        w_loaded = sem("w_loaded")
        late_loaded = sem("late_loaded")
        x_parts = [sem(f"x_parts{i}") for i in range(4)]
        rows_loaded = [sem(f"rows_loaded{i}") for i in range(NA)]
        mask_loaded = [sem(f"mask_loaded{i}") for i in range(2)]
        mask_stored = [sem(f"mask_stored{i}") for i in range(NM)]
        x_again = sem("x_again")
        out_stored = sem("out_stored")
        consts = sem("consts")
        order_dve = sem("order_dve")
        order_pool = sem("order_pool")
        order_act = sem("order_act")
        var_ready = sem("var_ready")
        root_ready = sem("root_ready")
        rstd_ready = sem("rstd_ready")
        norm_done = sem("norm_done")
        tr_done = sem("tr_done")
        tr_hi = sem("tr_hi")
        tr_used = sem("tr_used")
        w_split = sem("w_split")
        w1_tr = sem("w1_tr")
        w1_used = sem("w1_used")
        mask_raw = sem("mask_raw")
        mask_built = sem("mask_built")
        maskT_filled = sem("maskT_filled")
        maskT_act = sem("maskT_act")
        maskT_dve = sem("maskT_dve")
        aux_ready = sem("aux_ready")
        aux_done = sem("aux_done")
        packs_ready = sem("packs_ready")
        c_ready = sem("c_ready")
        proj_begun = sem("proj_begun")
        max_begun = sem("max_begun")
        scores_ready = sem("scores_ready")
        exp_done = sem("exp_done")
        hi_done = sem("hi_done")
        lo_dve = sem("lo_dve")
        lo_pool = sem("lo_pool")
        pv_done = sem("pv_done")
        acc_used = sem("acc_used")
        heads_done = sem("heads_done")
        ot_filled = sem("ot_filled")
        ot_ready = sem("ot_ready")
        wo_done = sem("wo_done")
        x2_done = sem("x2_done")
        g_norm = sem("g_norm")
        g_hi = sem("g_hi")
        g_ready = sem("g_ready")
        adjT_ready = sem("adjT_ready")
        x2b_ready = sem("x2b_ready")
        agg_done = sem("agg_done")
        agg_ready = sem("agg_ready")
        y_done = sem("y_done")
        y_ready = sem("y_ready")

        block = ctx.enter_context(nc.Block())
        NC = 5

        @block.sync
        def _(sp):
            for i in range(4):
                part = slice(i * NT // 4, (i + 1) * NT // 4)
                sp.dma_start(x_in[:, part, :], x_rows[:, part, :]).then_inc(x_parts[i], 16)
            for t in range(KT):
                for src, c in ((Wqs, 0), (Wks, KD)):
                    sp.dma_start(wqk_in[:, t, :, c:c + KD],
                                 src[:, t * P:(t + 1) * P, :].rearrange("h p k -> p h k")).then_inc(w_loaded, 16)
                sp.dma_start(wv_in[:, t, :].rearrange("p (h k) -> p h k", h=H),
                             Wvs[:, t * P:(t + 1) * P, :].rearrange("h p k -> p h k")).then_inc(w_loaded, 16)

            def store_mask(t):
                sp.wait_ge(mask_built, t + 1)
                sp.dma_start(mask_dram[t], mask_buf(t)[:, :]).then_inc(mask_stored[t % NM], 16)

            for t in range(NT):
                if t >= NA:
                    sp.wait_ge(mask_raw, t - NA + 1)
                sp.dma_start(rows_in[:, t % NA, :], adj_rows[t]).then_inc(rows_loaded[t % NA], 16)
                if t >= NA:
                    store_mask(t - NA)
            for t in range(NT - NA, NT):
                store_mask(t)
            masks_stored(sp)
            sp.wait_ge(maskT_filled, NT)
            sp.wait_ge(aux_done, 2 * job(0, "max", 2 * NT - 1) + 2)

            def mask_rows(h):
                for t in range(NT):
                    if t >= 2:
                        sp.wait_ge(aux_done, 2 * job(h, "max", 2 * t - 3) + 2)
                    elif not (isinstance(h, int) and h == 1):
                        sp.wait_ge(aux_done, 2 * job(h - 1, "max", 2 * (NT + t) - 3) + 2)
                    sp.dma_start(mask_row[:, t % 2, :], mask_dram[t]).then_inc(mask_loaded[t % 2], 16)

            mask_rows(1)
            with sp.Fori(0, (H - 2) // 2) as i:
                mask_rows(2 * i + 2)
                mask_rows(2 * i + 3)
            sp.wait_ge(scores_ready, (H - 1) * ST)
            sp.dma_start(x2, x_rows).then_inc(x_again, 16)
            sp.wait_ge(aux_done, 2 * job(H - 1, "max", 0) + 2)
            sp.dma_start(wo, Wo.rearrange("h k d -> (h k) d").rearrange("(c p) d -> p c d", p=P))\
                .then_inc(late_loaded, 16)
            sp.dma_start(w1_in, W1.rearrange("(t p) d -> p t d", p=P)).then_inc(late_loaded, 16)
            sp.dma_start(bias, b1.rearrange("(a d) -> a d", a=1).to_broadcast([P, D])).then_inc(late_loaded, 16)
            for t in range(NT):
                sp.wait_ge(y_ready, t + 1)
                sp.dma_start(out_rows[:, t, :], x2[:, t, :]).then_inc(out_stored, 16)
            sp.wait_ge(out_stored, 16 * NT)

        @block.gpsimd
        def _(pool):
            g = nc.gpsimd
            g.memset(id32[:, :], 0.0).then_inc(order_pool, 1)
            g.memset(diag_floor[:, :], -BIG).then_inc(order_pool, 1)
            pool.wait_ge(order_pool, 2)
            g.affine_select(out=id32[:, :], in_=id32[:, :], compare_op=ALU.not_equal, fill=1.0,
                            base=0, pattern=[[-1, P]], channel_multiplier=1).then_inc(consts, 1)
            g.affine_select(out=diag_floor[:, :], in_=diag_floor[:, :], compare_op=ALU.not_equal,
                            fill=DIAG_EPS, base=0, pattern=[[-1, P]], channel_multiplier=1).then_inc(consts, 1)
            pool.wait_ge(consts, 2)
            g.tensor_copy(id16[:, :], id32[:, :]).then_inc(consts, 1)
            g.tensor_copy(idb[:, :], id32[:, :]).then_inc(consts, 1)
            g.tensor_scalar(mask_id[:, :], id32[:, :], MASK_STEP, None, ALU.mult).then_inc(consts, 1)

            def low_parts(h):
                for s in range(ST):
                    if pool_step(s):
                        pool.wait_ge(hi_done, h * ST + s + 1)
                        g.tensor_tensor(prob_lo(s), prob(s), prob_hi(s), ALU.subtract).then_inc(lo_pool, 1)

            masks_stored(pool)
            pool.wait_ge(maskT_filled, NT)
            pool.wait_ge(aux_done, 2 * job(0, "max", 2 * NT - 1) + 2)
            g.memset(packs[64:65, 1, 1, :], -1.0).then_inc(order_pool, 1)
            pool.wait_ge(order_pool, 3)
            low_parts(0)
            with pool.Fori(0, (H - 2) // 2) as i:
                low_parts(2 * i + 1)
                low_parts(2 * i + 2)
            low_parts(H - 1)
            pool.wait_ge(late_loaded, 48)
            for b in range(NB):
                pool.wait_ge(g_norm, b + 1)
                rows = x2[:, b * TB:(b + 1) * TB, :]
                g.tensor_tensor(rows, rows, bias.rearrange("p (o d) -> p o d", o=1).to_broadcast([P, TB, D]),
                                ALU.add).then_inc(x2b_ready, 1)

        @block.scalar
        def _(act):
            a = nc.scalar
            for half in range(2):
                cols = slice(half * NT // 2, (half + 1) * NT // 2)
                act.wait_ge(var_ready, half + 1)
                a.activation(root[:, cols], ve[:, cols], ACT.Sqrt).then_inc(root_ready, 1)

            def raw_mask(t):
                act.wait_ge(rows_loaded[t % NA], 16 * (t // NA + 1))
                if t >= NM:
                    act.wait_ge(mask_stored[t % NM], 16 * (t // NM))
                    act.wait_ge(maskT_filled, t - NM + 1)
                    act.wait_ge(aux_done, 2 * job(0, "max", 2 * (t - NM) + 1) + 2)
                a.activation(mask_buf(t)[:, :], rows_in[:, t % NA, :], ACT.Copy, scale=BIG, bias=-BIG,
                             accum_out=deg[:, t:t + 1]).then_inc(mask_raw, 1)

            def keep_mask_T(t):
                act.wait_ge(maskT_filled, t + 1)
                a.activation(mask_T[:, 0:MP, t * P:(t + 1) * P],
                             sc_bf(t)[:, 0:HALF].rearrange("p (m q) -> p m q", q=P), ACT.Copy).then_inc(maskT_act, 1)

            for t in range(NT):
                if t % 8 == 0:
                    act.wait_ge(rstd_ready, t // 8 + 1)
                last = a.activation(h_in[:, t, :], x_in[:, t, :], ACT.Relu,
                                    bias=shift[:, t:t + 1], scale=rstd[:, t:t + 1])
                if t % 8 == 7:
                    last.then_inc(norm_done, 1)
            for g in range(2 * KT):
                half, t = g // KT, g % KT
                act.wait_ge(tr_done, g + 1)
                a.activation(hT[:, 0, t, half * HALF:(half + 1) * HALF], group_ps(g), ACT.Copy).then_inc(tr_hi, 1)
                if g == KT - 1:
                    raw_mask(0)
            raw_mask(1)
            for t in range(2, NT + 2):
                if t < NT:
                    raw_mask(t)
                keep_mask_T(t - 2)

            def probabilities(h, first):
                for s in range(ST):
                    n = h * ST + s
                    act.wait_ge(scores_ready, n + 1)
                    if not first or s >= 2:
                        ps = s - 2 if s >= 2 else s - 2 + ST
                        dve_n, pool_n = lo_count(h if s >= 2 else h - 1, ps)
                        if pool_step(ps):
                            act.wait_ge(lo_pool, pool_n)
                        else:
                            act.wait_ge(lo_dve, dve_n)
                    a.activation(prob(s), sc_flat(s), ACT.Exp).then_inc(exp_done, 1)
                    if not first or s >= LAG_BUFS:
                        act.wait_ge(pv_done, n - LAG_BUFS + 1)
                    act.wait_ge(exp_done, n + 1)
                    a.activation(prob_hi(s), prob(s), ACT.Copy).then_inc(hi_done, 1)

            probabilities(0, True)
            with act.Fori(0, (H - 2) // 2) as i:
                probabilities(2 * i + 1, False)
                probabilities(2 * i + 2, False)
            probabilities(H - 1, False)

            act.wait_ge(var_ready, 3)
            a.activation(deg_root[:, :], dis[:, :], ACT.Sqrt).then_inc(root_ready, 1)
            act.wait_ge(pv_done, H * ST)
            act.wait_ge(w1_tr, 1)
            a.activation(w1T.rearrange("p a b -> p (a b)"), scores_ps[0][:, 1, :], ACT.Copy).then_inc(w1_used, 1)
            for t in range(NT):
                act.wait_ge(ot_filled, t + 1)
                if t >= 2:
                    act.wait_ge(wo_done, t - 1)
                a.activation(ot_sb(t), scores_ps[t % 2][:, 0, :], ACT.Copy).then_inc(ot_ready, 1)
                if t % TB == TB - 1:
                    b = t // TB
                    act.wait_ge(var_ready, 4 + b)
                    a.activation(root[:, b * TB:t + 1], ve[:, b * TB:t + 1], ACT.Sqrt).then_inc(root_ready, 1)
                if t % TB == 2 and t > TB or t == NT - 1:
                    for b in ([t // TB - 1] if t < NT - 1 else [NB - 1]):
                        act.wait_ge(rstd_ready, 3 + b)
                        if b >= 2:
                            act.wait_ge(g_ready, b - 1)
                        for u in range(TB):
                            k = b * TB + u
                            last = a.activation(g_f(b)[:, u * D:(u + 1) * D], x2[:, k, :], ACT.Relu,
                                                bias=shift[:, k:k + 1], scale=rstd[:, k:k + 1])
                        last.then_inc(g_norm, 1)
                        act.wait_ge(g_norm, b + 1)
                        a.activation(g_split[:, b * TB:(b + 1) * TB, 0, :],
                                     g_f(b).rearrange("p (t d) -> p t d", d=D), ACT.Copy).then_inc(g_hi, 1)
            for b in range(NB):
                act.wait_ge(agg_done, b + 1)
                if b < 2:
                    act.wait_ge(g_ready, NB)
                else:
                    act.wait_ge(y_done, TB * (b - 1))
                a.activation(agg_sb(b), sc_flat(b), ACT.Copy).then_inc(agg_ready, 1)

        @block.vector
        def _(dve):
            v = nc.vector
            chain = {"base": 0, "n": 0}

            def link(ins):
                chain["n"] += 1
                return ins.then_inc(order_dve, 1)

            def settle():
                dve.wait_ge(order_dve, chain["base"] + chain["n"])

            def newton_rsqrt(y, r, value, w):
                link(v.reciprocal(y, r))
                settle()
                link(v.tensor_tensor(w, y, y, ALU.mult))
                settle()
                link(v.tensor_tensor(w, w, value, ALU.mult))
                settle()
                link(v.tensor_scalar(w, w, -0.5, 1.5, ALU.mult, ALU.add))
                settle()
                link(v.tensor_tensor(y, y, w, ALU.mult))
                settle()

            link(v.memset(packs[64:65, 0, 1, :], -1.0))
            for p in range(2):
                link(v.memset(values[:, p, :, 2 * KD:VW], 1.0))
            for half in range(2):
                cols = slice(half * NT // 2, (half + 1) * NT // 2)
                for t in range(half * NT // 2, (half + 1) * NT // 2):
                    if t % (NT // 4) == 0:
                        dve.wait_ge(x_parts[t // (NT // 4)], 16)
                    link(v.bn_stats(stats[:, t, :], x_in[:, t, :]))
                settle()
                for t in range(half * NT // 2, (half + 1) * NT // 2):
                    link(v.bn_aggr(mv[:, t, :], stats[:, t, :]))
                settle()
                v.tensor_scalar(ve[:, cols], mv[:, cols, 1], LN_EPS, None, ALU.add).then_inc(var_ready, 1)
                dve.wait_ge(root_ready, half + 1)
                newton_rsqrt(rstd[:, cols], root[:, cols], ve[:, cols], newton[:, cols])
                v.scalar_tensor_tensor(out=shift[:, cols], in0=mv[:, cols, 0], scalar=-1.0, in1=rstd[:, cols],
                                       op0=ALU.mult, op1=ALU.mult).then_inc(rstd_ready, 1)
            dve.wait_ge(w_loaded, 16 * 3 * KT)
            for src, dst, q in ((wqk_in[:, :, :, 0:KD], wqk[:, :, :, :, 0:KD], True),
                                (wqk_in[:, :, :, KD:2 * KD], wqk[:, :, :, :, KD:2 * KD], False),
                                (wv_in, wv[:, :, :, :], False)):
                scale = WS * KD ** -0.5 if q else WS
                for t in range(KT):
                    link(v.tensor_scalar(dst[:, 0, t], src[:, t], scale, None, ALU.mult))
                    settle()
                    link(v.scalar_tensor_tensor(out=dst[:, 1, t], in0=src[:, t], scalar=scale, in1=dst[:, 0, t],
                                                op0=ALU.mult, op1=ALU.subtract))
            settle()
            dve.sem_inc(w_split, 1)
            for g in range(2 * KT):
                half, t = g // KT, g % KT
                cols = slice(half * HALF, (half + 1) * HALF)
                dve.wait_ge(tr_hi, g + 1)
                v.tensor_tensor(hT[:, 1, t, cols], group_ps(g), hT[:, 0, t, cols], ALU.subtract).then_inc(tr_used, 1)

            def drain(h, kind, i, par, in_loop, masks_here=False):
                n = job(h, kind, i)
                if kind == "proj":
                    for c in range(2):
                        part = slice(c * QB, (c + 1) * QB)
                        dve.wait_ge(aux_ready, 2 * n + 1 + c)
                        link(v.tensor_scalar(split_hi[:, part], aux_ps[:, c, :], 1.0 / WS, None, ALU.mult))
                        settle()
                        v.scalar_tensor_tensor(out=split_lo[:, part], in0=aux_ps[:, c, :], scalar=1.0 / WS,
                                               in1=split_hi[:, part], op0=ALU.mult, op1=ALU.subtract)\
                            .then_inc(aux_done, 1)
                    cols = slice(i * HALF, (i + 1) * HALF)
                    dve.wait_ge(aux_done, 2 * n + 2)
                    if in_loop and i == 0 and not (isinstance(h, int) and h == 1):
                        dve.wait_ge(scores_ready, (h - 1) * ST)
                    v.tensor_copy(kA(par)[0:64, cols], split_hi[64:128, :])
                    v.tensor_copy(kA(par)[64:128, cols], split_hi[64:128, :])
                    v.tensor_copy(qA(par)[0:64, cols], split_hi[0:64, :])
                    v.tensor_copy(qA(par)[64:128, cols], split_lo[0:64, :])
                    v.tensor_copy(qB(par)[0:64, cols], split_hi[0:64, :])
                    v.tensor_copy(kB(par)[0:64, cols], split_lo[64:128, :]).then_inc(packs_ready, 1)
                    dve.wait_ge(packs_ready, 2 * h + i + 1)
                elif kind == "value":
                    vals = values[:, par, :, :]
                    src = aux_flat.rearrange("p (m k) -> p m k", k=KD)
                    if in_loop and not (isinstance(h, int) and h == 1):
                        dve.wait_ge(pv_done, (h - 1) * ST)
                    dve.wait_ge(aux_ready, 2 * n + 2)
                    link(v.tensor_scalar(vals[:, :, KD:2 * KD], src, 1.0 / WS, None, ALU.mult))
                    settle()
                    v.scalar_tensor_tensor(out=vals[:, :, 0:KD], in0=src, scalar=1.0 / WS,
                                           in1=vals[:, :, KD:2 * KD], op0=ALU.mult, op1=ALU.subtract)\
                        .then_inc(aux_done, 2)
                elif kind == "max":
                    t, half = i // 2, i % 2
                    if not masks_here and half == 0:
                        dve.wait_ge(mask_loaded[t % 2], 16 * ((h - 1) * (NT // 2) + t // 2 + 1))
                    rows = mask_buf(t)[:, :] if masks_here else mask_row[:, t % 2, :]
                    for c in range(2):
                        quarter = 2 * half + c
                        dve.wait_ge(aux_ready, 2 * n + 1 + c)
                        if in_loop:
                            dve.sem_inc(max_begun, 1)
                        v.tensor_tensor_reduce(out=junk[:, c * QB:(c + 1) * QB], in0=aux_ps[:, c, :],
                                               in1=rows[:, quarter * QB:(quarter + 1) * QB],
                                               scale=1.0, scalar=-3e38, op0=ALU.add, op1=ALU.max,
                                               accum_out=cmax[:, par, t, quarter:quarter + 1]).then_inc(aux_done, 1)
                    if i % (4 * TB) == 4 * TB - 1:
                        tiles = slice(i // (4 * TB) * 2 * TB, (i // (4 * TB) + 1) * 2 * TB)
                        dve.wait_ge(aux_done, 2 * n + 2)
                        v.tensor_reduce(out=c16[:, par, tiles], in_=cmax[:, par, tiles, :],
                                        axis=mybir.AxisListType.X, op=ALU.max).then_inc(c_ready, 1)
                else:
                    dve.wait_ge(aux_ready, 2 * n + 2)
                    v.tensor_copy(qB(par)[64:65, i * HALF:(i + 1) * HALF], aux_flat[0:1, :]).then_inc(aux_done, 2)

            dve.wait_ge(consts, NC)

            def finish_mask(t):
                blk = mask_buf(t)[:, t * P:(t + 1) * P]
                dve.wait_ge(mask_raw, t + 1)
                if t >= 1:
                    dve.wait_ge(mask_built, t)
                link(v.tensor_tensor_reduce(out=o_sum[:, 0:P // KD, :].rearrange("p t k -> p (t k)"), in0=blk,
                                            in1=id32[:, :], scale=1.0, scalar=0.0, op0=ALU.mult, op1=ALU.add,
                                            accum_out=adj_diag[:, t:t + 1]))
                settle()
                v.tensor_tensor(blk, blk, diag_floor[:, :], ALU.max).then_inc(mask_built, 1)

            def keep_mask_T(t):
                dve.wait_ge(maskT_filled, t + 1)
                v.tensor_copy(mask_T[:, MP:NT, t * P:(t + 1) * P],
                              sc_bf(t)[:, HALF:2 * HALF].rearrange("p (m q) -> p m q", q=P)).then_inc(maskT_dve, 1)

            finish_mask(0)
            for t, (kind, i) in enumerate(JOBS[0:3]):
                finish_mask(t + 1)
                if t >= 1:
                    keep_mask_T(t - 1)
                drain(0, kind, i, 0, False)
            for t in range(3, NT + 1):
                before, after = head0_jobs(t)
                if t + 1 < NT:
                    finish_mask(t + 1)
                for kind, i in before:
                    drain(0, kind, i, 0, False, masks_here=True)
                keep_mask_T(t - 1)
                for kind, i in after:
                    drain(0, kind, i, 0, False, masks_here=True)
            masks_stored(dve)

            def evacuate(h, b):
                settle()
                link(v.reciprocal(o_rec[:, :], acc[:, :, 2 * KD]))
                link(v.tensor_copy(o_lo[:, :, :], acc[:, :, 0:KD]))
                settle()
                v.tensor_tensor(o_sum[:, :, :], acc[:, :, KD:2 * KD], o_lo[:, :, :], ALU.add).then_inc(acc_used, 1)
                dve.wait_ge(acc_used, NB * h + b + 1)
                link(v.tensor_tensor(heads_out[:, b * TB:(b + 1) * TB, bass.ds(h * KD, KD)], o_sum[:, :, :],
                                     o_rec[:, :].rearrange("p (t o) -> p t o", o=1).to_broadcast([P, TB, KD]),
                                     ALU.mult))

            LINKS = 3 * NB + 5
            links0 = chain["n"]

            def period(h, par, first, last):
                if not first:
                    chain["base"], chain["n"] = LINKS * h + (links0 - 3), 0
                def low(hh, st):
                    if not pool_step(st):
                        dve.wait_ge(hi_done, hh * ST + st + 1)
                        v.tensor_tensor(prob_lo(st), prob(st), prob_hi(st), ALU.subtract).then_inc(lo_dve, 1)

                def drains(slot):
                    for kind, i in at_slot[slot]:
                        if (kind, i) == CROW_LAST:
                            drain(h, kind, i, par, True)
                        elif not last:
                            drain(h + 1, kind, i, 1 - par, True)

                for s in range(ST):
                    drains(4 * s)
                    if s >= 1:
                        low(h, s - 1)
                    drains(4 * s + 1)
                    drains(4 * s + 2)
                    if (s - LAG) % MP == MP - 1 and s >= LAG:
                        dve.wait_ge(pv_done, h * ST + s - LAG + 1)
                        evacuate(h, (s - LAG) // MP)
                    if s == LAG - 1 and not first:
                        dve.wait_ge(pv_done, h * ST)
                        evacuate(h - 1, NB - 1)
                    drains(4 * s + 3)
                low(h, ST - 1)
                if not last:
                    want = LINKS - (3 if first else 0)
                    assert chain["n"] - (links0 if first else 0) == want, (chain["n"], want)

            period(0, 0, True, False)
            with dve.Fori(0, (H - 2) // 2) as i:
                period(2 * i + 1, 1, False, False)
                period(2 * i + 2, 0, False, False)
            period(H - 1, 1, False, True)
            dve.wait_ge(pv_done, H * ST)
            evacuate(H - 1, NB - 1)
            settle()
            dve.sem_inc(heads_done, 1)

            link(v.tensor_scalar(adj_diag[:, :], adj_diag[:, :], 1.0 / BIG, None, ALU.mult))
            link(v.tensor_scalar(deg[:, :], deg[:, :], 1.0 / BIG, float(N), ALU.mult, ALU.add))
            settle()
            link(v.tensor_scalar(dis[:, :], deg[:, :], DEG_EPS, None, ALU.add))
            settle()
            dve.sem_inc(var_ready, 1)
            for t in range(NT):
                link(v.tensor_scalar(mask_T[:, t, :], mask_T[:, t, :], 1.0 / BIG, 1.0, ALU.mult, ALU.add))
            settle()
            for t in range(NT):
                blk = mask_T[:, t, t * P:(t + 1) * P]
                v.scalar_tensor_tensor(out=blk, in0=idb[:, :], scalar=adj_diag[:, t:t + 1], in1=blk,
                                       op0=ALU.mult, op1=ALU.add).then_inc(adjT_ready, 1)
            dve.wait_ge(root_ready, 3)
            link(v.tensor_copy(ve[:, :], dis[:, :]))
            settle()
            newton_rsqrt(dis[:, :], deg_root[:, :], ve[:, :], newton[:, :])
            dve.wait_ge(x_again, 16)
            for t in range(NT):
                dve.wait_ge(wo_done, t + 1)
                link(v.tensor_tensor(x2[:, t, :], x2[:, t, :], aux_ps[:, t % 2, 0:D], ALU.add))
                settle()
                dve.sem_inc(x2_done, 1)
                link(v.bn_stats(stats[:, t, :], x2[:, t, :]))
                settle()
                link(v.bn_aggr(mv[:, t, :], stats[:, t, :]))
                if t % TB == TB - 1:
                    b = t // TB
                    cols = slice(b * TB, t + 1)
                    settle()
                    link(v.tensor_scalar(ve[:, cols], mv[:, cols, 1], LN_EPS, None, ALU.add))
                    settle()
                    dve.sem_inc(var_ready, 1)
                    dve.wait_ge(root_ready, 4 + b)
                    newton_rsqrt(rstd[:, cols], root[:, cols], ve[:, cols], newton[:, cols])
                    link(v.scalar_tensor_tensor(out=rstd[:, cols], in0=rstd[:, cols], scalar=0.25, in1=dis[:, cols],
                                                op0=ALU.mult, op1=ALU.mult))
                    settle()
                    link(v.scalar_tensor_tensor(out=shift[:, cols], in0=mv[:, cols, 0], scalar=-1.0,
                                                in1=rstd[:, cols], op0=ALU.mult, op1=ALU.mult))
                    settle()
                    dve.sem_inc(rstd_ready, 1)
                if t % TB == TB - 1 and t >= 2 * TB - 1 or t == NT - 1:
                    for b in ([t // TB - 1] + ([NB - 1] if t == NT - 1 else [])):
                        dve.wait_ge(g_hi, b + 1)
                        v.tensor_tensor(g_split[:, b * TB:(b + 1) * TB, 1, :],
                                        g_f(b).rearrange("p (t d) -> p t d", d=D),
                                        g_split[:, b * TB:(b + 1) * TB, 0, :], ALU.subtract).then_inc(g_ready, 1)
            link(v.tensor_scalar(dis[:, :], dis[:, :], 4.0, None, ALU.mult))
            settle()
            dve.wait_ge(x2b_ready, NB)
            for t in range(NT):
                dve.wait_ge(y_done, t + 1)
                v.scalar_tensor_tensor(out=x2[:, t, :], in0=acc_ps[:, t % 2, 0:D], scalar=dis[:, t:t + 1],
                                       in1=x2[:, t, :], op0=ALU.mult, op1=ALU.add).then_inc(y_ready, 1)

        @block.tensor
        def _(pe):
            m = nc.tensor
            pe.wait_ge(consts, NC)
            for g in range(2 * KT):
                half, t = g // KT, g % KT
                if t == 0:
                    pe.wait_ge(norm_done, half + 1)
                for u in range(8):
                    last = m.transpose(group_ps(g)[:, u * P:(u + 1) * P], h_in[:, half * 8 + u, t * P:(t + 1) * P],
                                       id32[:, :])
                last.then_inc(tr_done, 1)
            pe.wait_ge(w_split, 1)
            pe.wait_ge(tr_used, 2 * KT)

            TERMS = ((0, 0), (1, 0), (0, 1))

            def fill(h, kind, i, par, in_loop):
                n = job(h, kind, i)
                if kind == "max" and i == 0:
                    pe.wait_ge(packs_ready, 2 * h + 2)
                if kind == "crow":
                    pe.wait_ge(c_ready, NB // 2 * h + i + 1)
                def bank(c):
                    if in_loop or n >= 1:
                        pe.wait_ge(aux_done, 2 * n - 1 + c)

                if kind == "proj":
                    for c in range(2):
                        bank(c)
                        if in_loop:
                            pe.sem_inc(proj_begun, 1)
                        cols = slice(i * HALF + c * QB, i * HALF + (c + 1) * QB)
                        steps = [(t, wp, hp) for t in range(KT) for wp, hp in TERMS]
                        for k, (t, wp, hp) in enumerate(steps):
                            weights = wqk[:, wp, t, :, :].rearrange("p h c -> p (h c)")
                            last = m.matmul(aux_ps[:, c, :], weights[:, bass.ds(h * 2 * KD, 2 * KD)],
                                            hT[:, hp, t, cols], start=(k == 0), stop=(k == len(steps) - 1))
                        last.then_inc(aux_ready, 1)
                elif kind == "value":
                    bank(1)
                    for u in range(NT):
                        steps = [(t, wp, hp) for t in range(KT) for wp, hp in TERMS]
                        for k, (t, wp, hp) in enumerate(steps):
                            last = m.matmul(aux_flat[:, u * KD:(u + 1) * KD], hT[:, hp, t, u * P:(u + 1) * P],
                                            wv[:, wp, t, bass.ds(h * KD, KD)],
                                            start=(k == 0), stop=(k == len(steps) - 1))
                    last.then_inc(aux_ready, 2)
                elif kind == "max":
                    t, half = i // 2, i % 2
                    for c in range(2):
                        k0 = half * HALF + c * QB
                        bank(c)
                        m.matmul(aux_ps[:, c, :], qA(par)[:, t * P:(t + 1) * P], kA(par)[:, k0:k0 + QB],
                                 start=True, stop=True).then_inc(aux_ready, 1)
                else:
                    bank(1)
                    for u in range(2 * TB):
                        t = i * 2 * TB + u
                        last = m.matmul(aux_flat[0:1, u * P:(u + 1) * P], c16[:, par, t:t + 1],
                                        id16[:, :], start=True, stop=True)
                    last.then_inc(aux_ready, 2)

            def transpose_mask(t):
                pe.wait_ge(mask_built, t + 1)
                if t >= 2:
                    pe.wait_ge(maskT_act, t - 1)
                    pe.wait_ge(maskT_dve, t - 1)
                for u in range(NT):
                    last = m.transpose(sc_bf(t)[:, u * P:(u + 1) * P], mask_buf(t)[:, u * P:(u + 1) * P],
                                       idb[:, :])
                last.then_inc(maskT_filled, 1)

            for t, (kind, i) in enumerate(JOBS[0:3]):
                transpose_mask(t)
                fill(0, kind, i, 0, False)
            for t in range(3, NT + 1):
                before, after = head0_jobs(t)
                for kind, i in before:
                    fill(0, kind, i, 0, False)
                if t < NT:
                    transpose_mask(t)
                for kind, i in after:
                    fill(0, kind, i, 0, False)
            pe.wait_ge(maskT_act, NT)
            pe.wait_ge(maskT_dve, NT)

            def scores(h, s, par, first, a):
                b, pair = s // MP, s % MP
                if s % (2 * MP) == 0 and a == 0:
                    pe.wait_ge(aux_done, 2 * job(h, "crow", b // 2) + 2)
                if a == 0 and (not first or s >= 2):
                    pe.wait_ge(exp_done, h * ST + s - 1)
                q = slice(b * QB, (b + 1) * QB)
                t = 2 * pair + a
                k = slice(t * P, (t + 1) * P)
                dst = scores_ps[s % 2][:, a, :]
                m.matmul(dst, kA(par)[:, k], qA(par)[:, q], start=True, stop=False)
                m.matmul(dst, kB(par)[0:65, k], qB(par)[0:65, q], start=False, stop=False)
                last = m.matmul(dst, mask_id[:, :], mask_T[:, t, q], start=False, stop=True)
                if a == 1:
                    last.then_inc(scores_ready, 1)

            def weigh(h, s, par, first, a):
                b, pair = s // MP, s % MP
                dve_n, pool_n = lo_count(h, s)
                if a == 0 and pool_step(s):
                    pe.wait_ge(lo_pool, pool_n)
                elif a == 0:
                    pe.wait_ge(lo_dve, dve_n)
                if pair == 0 and a == 0 and not (first and b == 0):
                    pe.wait_ge(acc_used, NB * h + b)
                t = 2 * pair + a
                for u in range(TB):
                    cols = slice(a * QB + u * P, a * QB + (u + 1) * P)
                    m.matmul(acc[:, u, 0:VW], prob_hi(s)[:, cols], values[:, par, t, :],
                             start=(t == 0 and u % 2 == 0), stop=False, skip_group_check=True)
                    last = m.matmul(acc[:, u, KD:VW], prob_lo(s)[:, cols], values[:, par, t, KD:VW],
                                    start=False, stop=(t == NT - 1), skip_group_check=True)
                if a == 1:
                    last.then_inc(pv_done, 1)

            def period(h, par, first, last):
                def fills(slot):
                    for kind, i in at_slot[slot]:
                        if (kind, i) == CROW_LAST:
                            fill(h, kind, i, par, True)
                        elif not last:
                            fill(h + 1, kind, i, 1 - par, True)

                for s in range(ST):
                    for a in range(2):
                        scores(h, s, par, first, a)
                        fills(4 * s + a)
                    for a in range(2):
                        if s >= LAG:
                            weigh(h, s - LAG, par, first, a)
                        elif not first:
                            weigh(h - 1, ST + s - LAG, 1 - par, False, a)
                        fills(4 * s + 2 + a)

            period(0, 0, True, False)
            with pe.Fori(0, (H - 2) // 2) as i:
                period(2 * i + 1, 1, False, False)
                period(2 * i + 2, 0, False, False)
            period(H - 1, 1, False, True)
            for s in range(ST - LAG, ST):
                for a in range(2):
                    weigh(H - 1, s, 1, False, a)

            pe.wait_ge(late_loaded, 48)
            pe.wait_ge(exp_done, H * ST)
            for t in range(KT):
                for u in range(KT):
                    last = m.transpose(scores_ps[0][:, 1, t * D + u * P:t * D + (u + 1) * P],
                                       w1_in[:, u, t * P:(t + 1) * P], id32[:, :])
            last.then_inc(w1_tr, 1)
            pe.wait_ge(w1_used, 1)
            pe.wait_ge(heads_done, 1)
            for t in range(NT + 1):
                if t < NT:
                    if t >= 2:
                        pe.wait_ge(ot_ready, t - 1)
                    for c in range(CT):
                        last = m.transpose(scores_ps[t % 2][:, 0, c * P:(c + 1) * P],
                                           heads_out[:, t, c * P:(c + 1) * P], id32[:, :])
                    last.then_inc(ot_filled, 1)
                if t >= 1:
                    k = t - 1
                    pe.wait_ge(ot_ready, k + 1)
                    if k >= 2:
                        pe.wait_ge(x2_done, k - 1)
                    for c in range(CT):
                        last = m.matmul(aux_ps[:, k % 2, 0:D], ot_sb(k)[:, c * P:(c + 1) * P], wo[:, c, :],
                                        start=(c == 0), stop=(c == CT - 1))
                    last.then_inc(wo_done, 1)

            pe.wait_ge(adjT_ready, NT)
            pe.wait_ge(g_ready, NB)

            def aggregate(b):
                if b >= 2:
                    pe.wait_ge(agg_ready, b - 1)
                for c in range(KT):
                    for t in range(NT):
                        for part in range(2):
                            last = m.matmul(scores_ps[b % 2][:, c, :], g_split[:, t, part, c * P:(c + 1) * P],
                                            mask_T[:, t, b * QB:(b + 1) * QB],
                                            start=(t == 0 and part == 0), stop=(t == NT - 1 and part == 1))
                last.then_inc(agg_done, 1)

            def transform(b):
                pe.wait_ge(agg_ready, b + 1)
                for u in range(TB):
                    t = b * TB + u
                    if t >= 2:
                        pe.wait_ge(y_ready, t - 1)
                    for c in range(KT):
                        last = m.matmul(acc_ps[:, t % 2, 0:D],
                                        agg_sb(b)[:, c * QB + u * P:c * QB + (u + 1) * P],
                                        w1T[:, c, :], start=(c == 0), stop=(c == KT - 1))
                    last.then_inc(y_done, 1)

            aggregate(0)
            for b in range(1, NB):
                aggregate(b)
                transform(b - 1)
            transform(NB - 1)


def mask_constants():
    best = None
    for i in range(1024):
        step = 1 + i / 1024
        want = 0.01 / step
        unit = 2.0 ** (-7 - 7)
        if want < 2.0 ** -7:
            unit /= 2
        eps = round(want / unit) * unit
        miss = abs(step * eps - 0.01)
        if best is None or miss < best[0]:
            best = (miss, step, eps)
    assert best[0] < 2e-8
    return best[1], best[2]


_INS = ['x', 'adj', 'L0_gnn_Wks', 'L0_gnn_Wqs', 'L0_gnn_Wvs', 'L0_gnn_Wo', 'L1_gnn_W', 'L1_gnn_b']
_OUTS = [((2048, 256), 'float32')]


def kernel(**inputs):
    import numpy as _np
    import concourse.bacc as _bacc
    from concourse import mybir as _mybir
    from concourse.bass_utils import run_bass_kernel_spmd as _run

    nc = _bacc.Bacc("TRN2", target_bir_lowering=False, num_devices=1)
    arrays, args = {}, []
    for name in _INS:
        a = _np.ascontiguousarray(inputs[name])
        arrays[f"in_{name}_dram"] = a
        args.append(nc.dram_tensor(f"in_{name}_dram", a.shape, _mybir.dt.from_np(a.dtype), kind="ExternalInput").ap())
    for i, (shape, dtype) in enumerate(_OUTS):
        dt = _mybir.dt.from_np(_np.dtype(dtype))
        args.append(nc.dram_tensor(f"out_{i}_dram", shape, dt, kind="ExternalOutput").ap())
    adj_preln_kernel(nc, *args)
    r = _run(nc, [arrays], core_ids=[0])
    got = tuple(r.results[0][f"out_{i}_dram"] for i in range(len(_OUTS)))
    return got[0]
```

```python
import concourse.bass as bass
from concourse import mybir
from contextlib import ExitStack


LAG = 3
LAG_BUFS = 4
LEAD = 3
PIECES = (1.3, 1.3, 0.65, 0.65)
AHEAD = (1.3, 7.8, 14.3, 20.8)
SPACING = 0.99


def place_jobs(jobs, steps):
    places, at = [], 0.0
    for _ in range(steps):
        for piece in PIECES:
            at += piece
            places.append(at)
    rest = (at - AHEAD[-1] - 3.0) / (len(jobs) - len(AHEAD)) * SPACING
    out, p = [[] for _ in places], 0
    for n, job in enumerate(jobs):
        want = AHEAD[n] if n < len(AHEAD) else AHEAD[-1] + 3.0 + (n - len(AHEAD)) * rest
        while places[p] < want - 1e-6:
            p += 1
        out[p].append(job)
    return out


def aux_jobs(blocks, tiles_per_block, halves):
    jobs = [("proj", 0), ("proj", 1), ("value", 0)]
    rows = []
    for a in range(blocks * tiles_per_block * halves):
        jobs.append(("max", a))
        if (a + 1) % (2 * tiles_per_block * halves) == 0:
            rows.append((a + 2, (a + 1) // (2 * tiles_per_block * halves) - 1))
        if rows and a == rows[0][0]:
            jobs.append(("crow", rows.pop(0)[1]))
    assert [b for _, b in rows] == [blocks // 2 - 1]
    return jobs


def adj_preln_kernel(nc, x, adj, Wks, Wqs, Wvs, Wo, W1, b1, out):
    fp32 = mybir.dt.float32
    fp16 = mybir.dt.float16
    bf16 = mybir.dt.bfloat16
    ALU = mybir.AluOpType
    ACT = mybir.ActivationFunctionType

    N, D = x.shape
    H, _, KD = Wqs.shape
    P = 128
    NT = N // P
    KT = D // P
    HK = H * KD
    CT = HK // P
    QB = 512
    NB = N // QB
    TB = QB // P
    MP = NT // 2
    ST = NB * MP
    HALF = 1024
    LN_EPS, DEG_EPS = 1e-5, 1e-8
    BIG = float(2 ** 53)
    MASK_STEP, DIAG_EPS = mask_constants()
    WS = 64.0
    VW = 2 * KD + 1

    JOBS = aux_jobs(NB, TB, N // HALF)
    NJ = len(JOBS) + 1
    POS = {job: i for i, job in enumerate(JOBS)}
    CROW_LAST = ("crow", NB // 2 - 1)
    PERIOD = JOBS[:LEAD] + [CROW_LAST] + JOBS[LEAD:]

    def job(h, kind, i):
        if (kind, i) == CROW_LAST:
            return (h + 1) * NJ + (LEAD - 1 if not (isinstance(h, int) and h == H - 1) else -1)
        n = POS[(kind, i)]
        if isinstance(h, int) and h == 0:
            return n
        return h * NJ + n - (n < LEAD)

    at_slot = place_jobs(PERIOD, ST)

    def out_step(t):
        return MP + LAG + 1 + 2 * t
    IN_LOOP = (ST - MP - LAG - 1) // 2

    def out_tile(s):
        t = (s - out_step(0)) // 2
        return t if s >= out_step(0) and s % 2 == out_step(0) % 2 and t < NT else None

    RESTORE = {8: [(0, 0), (0, 1)], 10: [(0, 2), (0, 3)], 20: [(1, 0)], 22: [(1, 1)], 24: [(1, 2)],
               26: [(1, 3)], 28: [(2, 0)], 30: [(2, 1)]}
    RESTORE_LATE = [(2, 2), (2, 3)] + [(3, k) for k in range(NT // TB)]

    def head0_jobs(t):
        first = 0 if t == 3 else 2 * (t - 1)
        jobs = [n for n, (kind, i) in enumerate(JOBS) if kind == "max" and first <= i < 2 * t]
        lo, hi = jobs[0], jobs[-1] + 1
        if JOBS[lo - 1][0] == "crow":
            lo -= 1
        mine = JOBS[lo:hi]
        return mine[:1], mine[1:]

    def pool_step(s):
        return s % 2 == 1

    def lo_count(h, s):
        mine = sum(pool_step(k) for k in range(s + 1))
        total = sum(pool_step(k) for k in range(ST))
        return h * (ST - total) + (s + 1 - mine), h * total + mine

    adj_rows = adj.rearrange("(t p) m -> t p m", p=P)
    x_rows = x.rearrange("(t p) d -> p t d", p=P)
    out_rows = out.rearrange("(t p) d -> p t d", p=P)
    mask_dram = nc.dram_tensor("mask_rows", (NT, P, N), bf16, kind="Internal").ap()

    ctx = ExitStack()
    with ctx:
        def sb(name, shape, dt):
            return ctx.enter_context(nc.sbuf_tensor(name, shape, dt))

        def pb(name, shape, dt):
            return ctx.enter_context(nc.psum_tensor(name, shape, dt))

        def sem(name):
            return ctx.enter_context(nc.semaphore(name))

        mask_T = sb("mask_T", [P, NT, N], bf16)
        mask_row = sb("mask_row", [P, 2, N], bf16)
        packs = sb("packs", [P, 2, 4, N], fp16)
        split_hi = sb("split_hi", [P, HALF], fp16)
        split_lo = sb("split_lo", [P, HALF], fp16)
        values = sb("values", [P, 2, NT, VW], fp16)
        hT = sb("hT", [P, 2, KT, N], fp16)
        wqk = sb("wqk", [P, 2, KT, H, 2 * KD], fp16)
        wv = sb("wv", [P, 2, KT, HK], fp16)
        work = sb("work", [P, 6 * 1024], fp32)
        heads_out = sb("heads_out", [P, NT, HK], fp32)
        junk = sb("junk", [P, HALF], bf16)
        id32 = sb("id32", [P, P], fp32)
        id16 = sb("id16", [P, P], fp16)
        idb = sb("idb", [P, P], bf16)
        mask_id = sb("mask_id", [P, P], fp16)
        diag_floor = sb("diag_floor", [P, P], bf16)
        cmax = sb("cmax", [P, 2, NT, N // QB], fp32)
        c16 = sb("c16", [P, 2, NT], fp16)
        o_lo = sb("o_lo", [P, TB, KD], fp32)
        o_sum = sb("o_sum", [P, TB, KD], fp32)
        o_rec = sb("o_rec", [P, TB], fp32)
        stats = sb("stats", [P, NT, 6], fp32)
        mv = sb("mv", [P, NT, 2], fp32)
        ve = sb("ve", [P, NT], fp32)
        root = sb("root", [P, NT], fp32)
        rstd = sb("rstd", [P, NT], fp32)
        newton = sb("newton", [P, NT], fp32)
        shift = sb("shift", [P, NT], fp32)
        deg = sb("deg", [P, NT], fp32)
        deg_root = sb("deg_root", [P, NT], fp32)
        dis = sb("dis", [P, NT], fp32)
        adj_diag = sb("adj_diag", [P, NT], fp32)

        def kA(p): return packs[:, p, 0, :]
        def kB(p): return packs[:, p, 1, :]
        def qA(p): return packs[:, p, 2, :]
        def qB(p): return packs[:, p, 3, :]

        def prob(s): return work[:, 1024 * (s % 2):1024 * (s % 2) + 1024]
        def prob_hi(s): return work[:, 2048 + 512 * (s % LAG_BUFS):2560 + 512 * (s % LAG_BUFS)].bitcast(fp16)
        def prob_lo(s): return work[:, 4096 + 512 * (s % LAG_BUFS):4608 + 512 * (s % LAG_BUFS)].bitcast(fp16)

        x_in = work[:, 0:NT * D].rearrange("p (t d) -> p t d", d=D)
        h_in = x_in
        wqk_in = work[:, NT * D:NT * D + KT * HK * 2].rearrange("p (t h c) -> p t h c", t=KT, h=H)
        NA = 3
        heads_flat = heads_out[:, :, :].rearrange("p t c -> p (t c)")
        rows_in = heads_flat[:, 0:NA * N].rearrange("p (b m) -> p b m", b=NA)
        wv_in = heads_flat[:, NA * N:NA * N + KT * HK].rearrange("p (t c) -> p t c", t=KT)
        NM = 6
        mask_packs = packs[:, 1, :, :].bitcast(bf16)

        def mask_buf(t):
            return mask_packs[:, t % NM, :] if t % NM < 4 else mask_row[:, t % NM - 4, :]

        def dve_keeps(t): return t >= 5 and t % 2 == 1
        def dve_kept(t): return sum(dve_keeps(k) for k in range(t + 1))

        def masks_stored(eng):
            for i in range(NM):
                eng.wait_ge(mask_stored[i], 16 * len(range(i, NT, NM)))

        late = wqk[:, :, :, :, :].rearrange("p a t h c -> p (a t h c)").bitcast(fp32)
        wo = late[:, 0:CT * D].rearrange("p (c d) -> p c d", d=D)
        w1_in = late[:, CT * D:(CT + KT) * D].rearrange("p (t d) -> p t d", d=D)
        bias = late[:, (CT + KT) * D:(CT + KT + 1) * D]
        w1T = wv[:, :, :, :].rearrange("p a t c -> p (a t c)").bitcast(fp32)[:, 0:KT * D]\
            .rearrange("p (t d) -> p t d", d=D)

        x2 = packs[:, 0, :, :].rearrange("p a n -> p (a n)").bitcast(fp32)\
            .rearrange("p (t d) -> p t d", d=D)
        g_split = hT[:, :, :, :].rearrange("p a b n -> p (a b n)")\
            .rearrange("p (t a d) -> p t a d", a=2, d=D)

        wo_parts = mask_row[:, 0, :].bitcast(fp16).rearrange("p (a c d) -> p a c d", a=2, d=D)
        even_values = values[:, 0, :, :].rearrange("p t c -> p (t c)")
        def o_parts(t): return even_values[:, 2 * HK * (t % 2):2 * HK * (t % 2 + 1)]
        def ot_sb(t): return (split_hi if t % 2 == 0 else split_lo)[:, :]

        def g_f(g): return work[:, 1024 * (g % 2):1024 * (g % 2) + 1024]
        def agg_sb(b): return work[:, 1024 * b + 2048:1024 * b + 3072]

        scores_ps = [pb(f"scores_ps{i}", [P, 2, QB], fp32) for i in range(2)]
        aux_ps = pb("aux_ps", [P, 2, QB], fp32)
        acc_ps = pb("acc_ps", [P, 2, QB], fp32)
        acc = acc_ps[:, :, :].rearrange("p b (j c) -> p (b j) c", c=QB // 2)
        aux_flat = aux_ps[:, :, :].rearrange("p b c -> p (b c)")
        acc_flat = acc_ps[:, :, :].rearrange("p b c -> p (b c)")

        ot_ps = aux_ps[:, 0, :].bitcast(fp16)
        wo_ps = aux_ps[:, 1, 0:D]

        def sc_flat(i): return scores_ps[i % 2][:, :, :].rearrange("p b c -> p (b c)")
        def group_ps(g):
            return (sc_flat(0), sc_flat(1), aux_flat, acc_flat)[g]

        def agg_ps(b):
            return (scores_ps[0], scores_ps[1], aux_ps, acc_ps)[b][:, :, :]

        def y_ps(t):
            return scores_ps[t // 2 % 2][:, t % 2, 0:D]

        def sc_bf(i): return sc_flat(i).bitcast(bf16)

        w_loaded = sem("w_loaded")
        late_loaded = sem("late_loaded")
        x_parts = [sem(f"x_parts{i}") for i in range(4)]
        rows_loaded = [sem(f"rows_loaded{i}") for i in range(NA)]
        mask_loaded = [sem(f"mask_loaded{i}") for i in range(2)]
        mask_stored = [sem(f"mask_stored{i}") for i in range(NM)]
        x_again = sem("x_again")
        out_stored = sem("out_stored")
        consts = sem("consts")
        order_dve = sem("order_dve")
        order_pool = sem("order_pool")
        var_ready = sem("var_ready")
        root_ready = sem("root_ready")
        rstd_ready = sem("rstd_ready")
        norm_done = sem("norm_done")
        tr_done = sem("tr_done")
        tr_hi = sem("tr_hi")
        tr_used = sem("tr_used")
        w_split = sem("w_split")
        w1_tr = sem("w1_tr")
        w1_used = sem("w1_used")
        mask_raw = sem("mask_raw")
        mask_built = sem("mask_built")
        maskT_filled = sem("maskT_filled")
        maskT_act = sem("maskT_act")
        maskT_dve = sem("maskT_dve")
        aux_ready = sem("aux_ready")
        aux_done = sem("aux_done")
        packs_ready = sem("packs_ready")
        c_ready = sem("c_ready")
        proj_begun = sem("proj_begun")
        max_begun = sem("max_begun")
        scores_ready = sem("scores_ready")
        exp_done = sem("exp_done")
        hi_done = sem("hi_done")
        lo_dve = sem("lo_dve")
        lo_pool = sem("lo_pool")
        pv_done = sem("pv_done")
        acc_used = sem("acc_used")
        wo_split = sem("wo_split")
        o_hi_ready = sem("o_hi_ready")
        o_lo_pool = sem("o_lo_pool")
        o_lo_dve = sem("o_lo_dve")
        ot_filled = sem("ot_filled")
        ot_dve = sem("ot_dve")
        ot_act = sem("ot_act")
        wo_done = sem("wo_done")
        x2_done = sem("x2_done")
        g_norm = sem("g_norm")
        g_hi = sem("g_hi")
        g_ready = sem("g_ready")
        adjT_ready = sem("adjT_ready")
        x2b_ready = sem("x2b_ready")
        agg_done = sem("agg_done")
        agg_ready = sem("agg_ready")
        y_done = sem("y_done")
        y_ready = sem("y_ready")

        block = ctx.enter_context(nc.Block())
        NC = 5

        @block.sync
        def _(sp):
            for i in range(4):
                part = slice(i * NT // 4, (i + 1) * NT // 4)
                sp.dma_start(x_in[:, part, :], x_rows[:, part, :]).then_inc(x_parts[i], 16)
            for t in range(KT):
                for src, c in ((Wqs, 0), (Wks, KD)):
                    sp.dma_start(wqk_in[:, t, :, c:c + KD],
                                 src[:, t * P:(t + 1) * P, :].rearrange("h p k -> p h k")).then_inc(w_loaded, 16)
                sp.dma_start(wv_in[:, t, :].rearrange("p (h k) -> p h k", h=H),
                             Wvs[:, t * P:(t + 1) * P, :].rearrange("h p k -> p h k")).then_inc(w_loaded, 16)

            def store_mask(t):
                sp.wait_ge(mask_built, t + 1)
                sp.dma_start(mask_dram[t], mask_buf(t)[:, :]).then_inc(mask_stored[t % NM], 16)

            for t in range(NT):
                if t >= NA:
                    sp.wait_ge(mask_raw, t - NA + 1)
                sp.dma_start(rows_in[:, t % NA, :], adj_rows[t]).then_inc(rows_loaded[t % NA], 16)
                if t >= NA:
                    store_mask(t - NA)
            for t in range(NT - NA, NT):
                store_mask(t)
            masks_stored(sp)
            sp.wait_ge(maskT_filled, NT)
            sp.wait_ge(aux_done, 2 * job(0, "max", 2 * NT - 1) + 2)

            def mask_rows(h):
                for t in range(NT):
                    if t >= 2:
                        sp.wait_ge(aux_done, 2 * job(h, "max", 2 * t - 3) + 2)
                    elif not (isinstance(h, int) and h == 1):
                        sp.wait_ge(aux_done, 2 * job(h - 1, "max", 2 * (NT + t) - 3) + 2)
                    sp.dma_start(mask_row[:, t % 2, :], mask_dram[t]).then_inc(mask_loaded[t % 2], 16)

            mask_rows(1)
            with sp.Fori(0, (H - 2) // 2) as i:
                mask_rows(2 * i + 2)
                mask_rows(2 * i + 3)
            sp.wait_ge(scores_ready, (H - 1) * ST)
            sp.dma_start(x2, x_rows).then_inc(x_again, 16)
            sp.wait_ge(aux_done, 2 * job(H - 1, "max", 0) + 2)
            sp.dma_start(wo, Wo.rearrange("h k d -> (h k) d").rearrange("(c p) d -> p c d", p=P))\
                .then_inc(late_loaded, 16)
            sp.dma_start(w1_in, W1.rearrange("(t p) d -> p t d", p=P)).then_inc(late_loaded, 16)
            sp.dma_start(bias, b1.rearrange("(a d) -> a d", a=1).to_broadcast([P, D])).then_inc(late_loaded, 16)
            for t in range(NT):
                sp.wait_ge(y_ready, t + 1)
                sp.dma_start(out_rows[:, t, :], x2[:, t, :]).then_inc(out_stored, 16)
            sp.wait_ge(out_stored, 16 * NT)

        @block.gpsimd
        def _(pool):
            g = nc.gpsimd
            g.memset(id32[:, :], 0.0).then_inc(order_pool, 1)
            g.memset(diag_floor[:, :], -BIG).then_inc(order_pool, 1)
            pool.wait_ge(order_pool, 2)
            g.affine_select(out=id32[:, :], in_=id32[:, :], compare_op=ALU.not_equal, fill=1.0,
                            base=0, pattern=[[-1, P]], channel_multiplier=1).then_inc(consts, 1)
            g.affine_select(out=diag_floor[:, :], in_=diag_floor[:, :], compare_op=ALU.not_equal,
                            fill=DIAG_EPS, base=0, pattern=[[-1, P]], channel_multiplier=1).then_inc(consts, 1)
            pool.wait_ge(consts, 2)
            g.tensor_copy(id16[:, :], id32[:, :]).then_inc(consts, 1)
            g.tensor_copy(idb[:, :], id32[:, :]).then_inc(consts, 1)
            g.tensor_scalar(mask_id[:, :], id32[:, :], MASK_STEP, None, ALU.mult).then_inc(consts, 1)

            def low_parts(h, last=False):
                for s in range(ST):
                    t = out_tile(s + 1)
                    if last and t is not None:
                        pool.wait_ge(o_hi_ready, t + 1)
                        g.tensor_tensor(o_parts(t)[:, HK:2 * HK], heads_out[:, t, :], o_parts(t)[:, 0:HK],
                                        ALU.subtract).then_inc(o_lo_pool, 1)
                    if pool_step(s):
                        pool.wait_ge(hi_done, h * ST + s + 1)
                        g.tensor_tensor(prob_lo(s), prob(s), prob_hi(s), ALU.subtract).then_inc(lo_pool, 1)

            masks_stored(pool)
            pool.wait_ge(maskT_filled, NT)
            pool.wait_ge(aux_done, 2 * job(0, "max", 2 * NT - 1) + 2)
            g.memset(packs[64:65, 1, 1, :], -1.0).then_inc(order_pool, 1)
            pool.wait_ge(order_pool, 3)
            low_parts(0)
            with pool.Fori(0, (H - 2) // 2) as i:
                low_parts(2 * i + 1)
                low_parts(2 * i + 2)
            low_parts(H - 1, True)
            pool.wait_ge(late_loaded, 48)
            for b in range(NB):
                pool.wait_ge(g_norm, b + 1)
                rows = x2[:, b * TB:(b + 1) * TB, :]
                g.tensor_tensor(rows, rows, bias.rearrange("p (o d) -> p o d", o=1).to_broadcast([P, TB, D]),
                                ALU.add).then_inc(x2b_ready, 1)

        @block.scalar
        def _(act):
            a = nc.scalar
            def raw_mask(t):
                act.wait_ge(rows_loaded[t % NA], 16 * (t // NA + 1))
                if t >= NM:
                    act.wait_ge(mask_stored[t % NM], 16 * (t // NM))
                    act.wait_ge(maskT_filled, t - NM + 1)
                    act.wait_ge(aux_done, 2 * job(0, "max", 2 * (t - NM) + 1) + 2)
                a.activation(mask_buf(t)[:, :], rows_in[:, t % NA, :], ACT.Copy, scale=BIG, bias=-BIG,
                             accum_out=deg[:, t:t + 1]).then_inc(mask_raw, 1)

            def keep_mask_T(t):
                act.wait_ge(maskT_filled, t + 1)
                n = MP if dve_keeps(t) else NT
                a.activation(mask_T[:, 0:n, t * P:(t + 1) * P],
                             sc_bf(t)[:, 0:n * P].rearrange("p (m q) -> p m q", q=P), ACT.Copy).then_inc(maskT_act, 1)

            for t in range(NT):
                if t % 8 == 0:
                    cols = slice(t, t + 8)
                    act.wait_ge(var_ready, t // 8 + 1)
                    a.activation(root[:, cols], ve[:, cols], ACT.Sqrt).then_inc(root_ready, 1)
                    act.wait_ge(rstd_ready, t // 8 + 1)
                last = a.activation(h_in[:, t, :], x_in[:, t, :], ACT.Relu,
                                    bias=shift[:, t:t + 1], scale=rstd[:, t:t + 1])
                if t % 8 == 7:
                    last.then_inc(norm_done, 1)
            for g in range(2 * KT):
                half, t = g // KT, g % KT
                act.wait_ge(tr_done, g + 1)
                a.activation(hT[:, 0, t, half * HALF:(half + 1) * HALF], group_ps(g), ACT.Copy).then_inc(tr_hi, 1)
                if g == KT - 1:
                    raw_mask(0)
            raw_mask(1)
            for t in range(2, NT + 2):
                if t < NT:
                    raw_mask(t)
                keep_mask_T(t - 2)

            def probabilities(h, first):
                for s in range(ST):
                    n = h * ST + s
                    act.wait_ge(scores_ready, n + 1)
                    if not first or s >= 2:
                        ps = s - 2 if s >= 2 else s - 2 + ST
                        dve_n, pool_n = lo_count(h if s >= 2 else h - 1, ps)
                        if pool_step(ps):
                            act.wait_ge(lo_pool, pool_n)
                        else:
                            act.wait_ge(lo_dve, dve_n)
                    a.activation(prob(s), sc_flat(s), ACT.Exp).then_inc(exp_done, 1)
                    if not first or s >= LAG_BUFS:
                        act.wait_ge(pv_done, n - LAG_BUFS + 1)
                    act.wait_ge(exp_done, n + 1)
                    a.activation(prob_hi(s), prob(s), ACT.Copy).then_inc(hi_done, 1)

            probabilities(0, True)
            with act.Fori(0, (H - 2) // 2) as i:
                probabilities(2 * i + 1, False)
                probabilities(2 * i + 2, False)
            probabilities(H - 1, False)

            def keep_heads_T(t):
                act.wait_ge(ot_filled, t + 1)
                act.wait_ge(wo_done, t - 1)
                a.activation(ot_sb(t), ot_ps, ACT.Copy).then_inc(ot_act, 1)

            def block_roots(n, first, end):
                cols = slice(first * TB, end * TB)
                act.wait_ge(var_ready, 4 + n)
                a.activation(root[:, cols], ve[:, cols], ACT.Sqrt).then_inc(root_ready, 1)

            def normalise(n, b):
                act.wait_ge(rstd_ready, 3 + n)
                if b >= 2:
                    act.wait_ge(g_ready, b - 1)
                for u in range(TB):
                    k = b * TB + u
                    last = a.activation(g_f(b)[:, u * D:(u + 1) * D], x2[:, k, :], ACT.Relu,
                                        bias=shift[:, k:k + 1], scale=rstd[:, k:k + 1])
                last.then_inc(g_norm, 1)
                act.wait_ge(g_norm, b + 1)
                a.activation(g_split[:, b * TB:(b + 1) * TB, 0, :],
                             g_f(b).rearrange("p (t d) -> p t d", d=D), ACT.Copy).then_inc(g_hi, 1)

            act.wait_ge(var_ready, 3)
            a.activation(deg_root[:, :], deg[:, :], ACT.Sqrt).then_inc(root_ready, 1)
            block_roots(0, 0, 2)
            dve_n, pool_n = lo_count(H - 1, ST - 1)
            act.wait_ge(lo_dve, dve_n)
            act.wait_ge(lo_pool, pool_n)
            normalise(0, 0)
            keep_heads_T(NT - 4)
            normalise(0, 1)
            block_roots(1, 2, 3)
            keep_heads_T(NT - 3)
            keep_heads_T(NT - 2)
            normalise(1, 2)
            keep_heads_T(NT - 1)
            block_roots(2, 3, 4)
            normalise(2, 3)
            for b in range(NB):
                act.wait_ge(agg_done, b + 1)
                a.activation(agg_sb(b), agg_ps(b).rearrange("p b c -> p (b c)"), ACT.Copy).then_inc(agg_ready, 1)

        @block.vector
        def _(dve):
            v = nc.vector
            chain = {"base": 0, "n": 0}

            def link(ins):
                chain["n"] += 1
                return ins.then_inc(order_dve, 1)

            def settle():
                dve.wait_ge(order_dve, chain["base"] + chain["n"])

            def newton_rsqrt(y, r, value, w):
                link(v.reciprocal(y, r))
                settle()
                link(v.tensor_tensor(w, y, y, ALU.mult))
                settle()
                link(v.tensor_tensor(w, w, value, ALU.mult))
                settle()
                link(v.tensor_scalar(w, w, -0.5, 1.5, ALU.mult, ALU.add))
                settle()
                link(v.tensor_tensor(y, y, w, ALU.mult))
                settle()

            link(v.memset(packs[64:65, 0, 1, :], -1.0))
            for p in range(2):
                link(v.memset(values[:, p, :, 2 * KD:VW], 1.0))
            for half in range(2):
                cols = slice(half * NT // 2, (half + 1) * NT // 2)
                for t in range(half * NT // 2, (half + 1) * NT // 2):
                    if t % (NT // 4) == 0:
                        dve.wait_ge(x_parts[t // (NT // 4)], 16)
                    link(v.bn_stats(stats[:, t, :], x_in[:, t, :]))
                settle()
                for t in range(half * NT // 2, (half + 1) * NT // 2):
                    link(v.bn_aggr(mv[:, t, :], stats[:, t, :]))
                settle()
                v.tensor_scalar(ve[:, cols], mv[:, cols, 1], LN_EPS, None, ALU.add).then_inc(var_ready, 1)
                dve.wait_ge(root_ready, half + 1)
                newton_rsqrt(rstd[:, cols], root[:, cols], ve[:, cols], newton[:, cols])
                v.scalar_tensor_tensor(out=shift[:, cols], in0=mv[:, cols, 0], scalar=-1.0, in1=rstd[:, cols],
                                       op0=ALU.mult, op1=ALU.mult).then_inc(rstd_ready, 1)
            dve.wait_ge(w_loaded, 16 * 3 * KT)
            def split_weights(src, dst, scale):
                for t in range(KT):
                    link(v.tensor_scalar(dst[:, 0, t], src[:, t], scale, None, ALU.mult))
                    settle()
                    link(v.scalar_tensor_tensor(out=dst[:, 1, t], in0=src[:, t], scalar=scale, in1=dst[:, 0, t],
                                                op0=ALU.mult, op1=ALU.subtract))

            split_weights(wqk_in[:, :, :, 0:KD], wqk[:, :, :, :, 0:KD], WS * KD ** -0.5)
            split_weights(wqk_in[:, :, :, KD:2 * KD], wqk[:, :, :, :, KD:2 * KD], WS)
            settle()
            dve.sem_inc(w_split, 1)
            for g in range(2 * KT):
                half, t = g // KT, g % KT
                cols = slice(half * HALF, (half + 1) * HALF)
                dve.wait_ge(tr_hi, g + 1)
                v.tensor_tensor(hT[:, 1, t, cols], group_ps(g), hT[:, 0, t, cols], ALU.subtract).then_inc(tr_used, 1)
            split_weights(wv_in, wv[:, :, :, :], WS)
            settle()
            dve.sem_inc(w_split, 1)

            def drain(h, kind, i, par, in_loop, masks_here=False):
                n = job(h, kind, i)
                if kind == "proj":
                    for c in range(2):
                        part = slice(c * QB, (c + 1) * QB)
                        dve.wait_ge(aux_ready, 2 * n + 1 + c)
                        link(v.tensor_scalar(split_hi[:, part], aux_ps[:, c, :], 1.0 / WS, None, ALU.mult))
                        settle()
                        v.scalar_tensor_tensor(out=split_lo[:, part], in0=aux_ps[:, c, :], scalar=1.0 / WS,
                                               in1=split_hi[:, part], op0=ALU.mult, op1=ALU.subtract)\
                            .then_inc(aux_done, 1)
                    cols = slice(i * HALF, (i + 1) * HALF)
                    dve.wait_ge(aux_done, 2 * n + 2)
                    if in_loop and i == 0 and not (isinstance(h, int) and h == 1):
                        dve.wait_ge(scores_ready, (h - 1) * ST)
                    v.tensor_copy(kA(par)[0:64, cols], split_hi[64:128, :])
                    v.tensor_copy(kA(par)[64:128, cols], split_hi[64:128, :])
                    v.tensor_copy(qA(par)[0:64, cols], split_hi[0:64, :])
                    v.tensor_copy(qA(par)[64:128, cols], split_lo[0:64, :])
                    v.tensor_copy(qB(par)[0:64, cols], split_hi[0:64, :])
                    v.tensor_copy(kB(par)[0:64, cols], split_lo[64:128, :]).then_inc(packs_ready, 1)
                    dve.wait_ge(packs_ready, 2 * h + i + 1)
                elif kind == "value":
                    vals = values[:, par, :, :]
                    src = aux_flat.rearrange("p (m k) -> p m k", k=KD)
                    if in_loop and not (isinstance(h, int) and h == 1):
                        dve.wait_ge(pv_done, (h - 1) * ST)
                    dve.wait_ge(aux_ready, 2 * n + 2)
                    link(v.tensor_scalar(vals[:, :, KD:2 * KD], src, 1.0 / WS, None, ALU.mult))
                    settle()
                    v.scalar_tensor_tensor(out=vals[:, :, 0:KD], in0=src, scalar=1.0 / WS,
                                           in1=vals[:, :, KD:2 * KD], op0=ALU.mult, op1=ALU.subtract)\
                        .then_inc(aux_done, 2)
                elif kind == "max":
                    t, half = i // 2, i % 2
                    if not masks_here and half == 0:
                        dve.wait_ge(mask_loaded[t % 2], 16 * ((h - 1) * (NT // 2) + t // 2 + 1))
                    rows = mask_buf(t)[:, :] if masks_here else mask_row[:, t % 2, :]
                    for c in range(2):
                        quarter = 2 * half + c
                        dve.wait_ge(aux_ready, 2 * n + 1 + c)
                        if in_loop:
                            dve.sem_inc(max_begun, 1)
                        v.tensor_tensor_reduce(out=junk[:, c * QB:(c + 1) * QB], in0=aux_ps[:, c, :],
                                               in1=rows[:, quarter * QB:(quarter + 1) * QB],
                                               scale=1.0, scalar=-3e38, op0=ALU.add, op1=ALU.max,
                                               accum_out=cmax[:, par, t, quarter:quarter + 1]).then_inc(aux_done, 1)
                    if i % (4 * TB) == 4 * TB - 1:
                        tiles = slice(i // (4 * TB) * 2 * TB, (i // (4 * TB) + 1) * 2 * TB)
                        dve.wait_ge(aux_done, 2 * n + 2)
                        v.tensor_reduce(out=c16[:, par, tiles], in_=cmax[:, par, tiles, :],
                                        axis=mybir.AxisListType.X, op=ALU.max).then_inc(c_ready, 1)
                else:
                    dve.wait_ge(aux_ready, 2 * n + 2)
                    v.tensor_copy(qB(par)[64:65, i * HALF:(i + 1) * HALF], aux_flat[0:1, :]).then_inc(aux_done, 2)

            dve.wait_ge(consts, NC)

            def finish_mask(t):
                blk = mask_buf(t)[:, t * P:(t + 1) * P]
                dve.wait_ge(mask_raw, t + 1)
                if t >= 1:
                    dve.wait_ge(mask_built, t)
                link(v.tensor_tensor_reduce(out=o_sum[:, 0:P // KD, :].rearrange("p t k -> p (t k)"), in0=blk,
                                            in1=id32[:, :], scale=1.0, scalar=0.0, op0=ALU.mult, op1=ALU.add,
                                            accum_out=adj_diag[:, t:t + 1]))
                settle()
                v.tensor_tensor(blk, blk, diag_floor[:, :], ALU.max).then_inc(mask_built, 1)

            def keep_mask_T(t):
                if not dve_keeps(t):
                    return
                dve.wait_ge(maskT_filled, t + 1)
                v.tensor_copy(mask_T[:, MP:NT, t * P:(t + 1) * P],
                              sc_bf(t)[:, HALF:2 * HALF].rearrange("p (m q) -> p m q", q=P)).then_inc(maskT_dve, 1)

            finish_mask(0)
            for t, (kind, i) in enumerate(JOBS[0:3]):
                finish_mask(t + 1)
                if t >= 1:
                    keep_mask_T(t - 1)
                drain(0, kind, i, 0, False)
            for t in range(3, NT + 1):
                before, after = head0_jobs(t)
                if t + 1 < NT:
                    finish_mask(t + 1)
                for kind, i in before:
                    drain(0, kind, i, 0, False, masks_here=True)
                keep_mask_T(t - 1)
                for kind, i in after:
                    drain(0, kind, i, 0, False, masks_here=True)
            masks_stored(dve)

            def evacuate(h, b):
                settle()
                link(v.reciprocal(o_rec[:, :], acc[:, :, 2 * KD]))
                link(v.tensor_copy(o_lo[:, :, :], acc[:, :, 0:KD]))
                settle()
                v.tensor_tensor(o_sum[:, :, :], acc[:, :, KD:2 * KD], o_lo[:, :, :], ALU.add).then_inc(acc_used, 1)
                dve.wait_ge(acc_used, NB * h + b + 1)
                link(v.tensor_tensor(heads_out[:, b * TB:(b + 1) * TB, bass.ds(h * KD, KD)], o_sum[:, :, :],
                                     o_rec[:, :].rearrange("p (t o) -> p t o", o=1).to_broadcast([P, TB, KD]),
                                     ALU.mult))

            def split_heads(t, both):
                settle()
                if t >= 2:
                    dve.wait_ge(ot_filled, t - 1)
                v.tensor_copy(o_parts(t)[:, 0:HK], heads_out[:, t, :]).then_inc(o_hi_ready, 1)
                if both:
                    dve.wait_ge(o_hi_ready, t + 1)
                    v.tensor_tensor(o_parts(t)[:, HK:2 * HK], heads_out[:, t, :], o_parts(t)[:, 0:HK],
                                    ALU.subtract).then_inc(o_lo_dve, 1)

            def keep_heads_T(t):
                dve.wait_ge(ot_filled, t + 1)
                if t >= 2:
                    dve.wait_ge(wo_done, t - 1)
                v.tensor_copy(ot_sb(t), ot_ps).then_inc(ot_dve, 1)

            def residual(t):
                dve.wait_ge(wo_done, t + 1)
                v.scalar_tensor_tensor(out=x2[:, t, :], in0=wo_ps, scalar=1.0 / WS, in1=x2[:, t, :],
                                       op0=ALU.mult, op1=ALU.add).then_inc(x2_done, 1)
                dve.wait_ge(x2_done, t + 1)
                link(v.bn_stats(stats[:, t, :], x2[:, t, :]))
                settle()
                link(v.bn_aggr(mv[:, t, :], stats[:, t, :]))

            def variances(first, end):
                cols = slice(first * TB, end * TB)
                settle()
                v.tensor_scalar(ve[:, cols], mv[:, cols, 1], LN_EPS, None, ALU.add).then_inc(var_ready, 1)

            def scales(n, first, end):
                cols = slice(first * TB, end * TB)
                dve.wait_ge(root_ready, 4 + n)
                newton_rsqrt(rstd[:, cols], root[:, cols], ve[:, cols], newton[:, cols])
                link(v.scalar_tensor_tensor(out=rstd[:, cols], in0=rstd[:, cols], scalar=0.25, in1=dis[:, cols],
                                            op0=ALU.mult, op1=ALU.mult))
                settle()
                v.scalar_tensor_tensor(out=shift[:, cols], in0=mv[:, cols, 0], scalar=-1.0, in1=rstd[:, cols],
                                       op0=ALU.mult, op1=ALU.mult).then_inc(rstd_ready, 1)

            def low_g(b):
                dve.wait_ge(g_hi, b + 1)
                v.tensor_tensor(g_split[:, b * TB:(b + 1) * TB, 1, :], g_f(b).rearrange("p (t d) -> p t d", d=D),
                                g_split[:, b * TB:(b + 1) * TB, 0, :], ALU.subtract).then_inc(g_ready, 1)

            def restore(b, k):
                if k == 0:
                    dve.wait_ge(scores_ready, (H - 1) * ST + (b + 1) * MP)
                part = mask_T[:, k * TB:(k + 1) * TB, b * QB:(b + 1) * QB]
                link(v.tensor_scalar(part, part, 1.0 / BIG, 1.0, ALU.mult, ALU.add))
                if k == NT // TB - 1:
                    settle()
                    for t in range(b * TB, (b + 1) * TB):
                        blk = mask_T[:, t, t * P:(t + 1) * P]
                        v.scalar_tensor_tensor(out=blk, in0=idb[:, :], scalar=adj_diag[:, t:t + 1], in1=blk,
                                               op0=ALU.mult, op1=ALU.add).then_inc(adjT_ready, 1)

            def last_head(s):
                if s == 6:
                    link(v.tensor_scalar(adj_diag[:, :], adj_diag[:, :], 1.0 / BIG, None, ALU.mult))
                    link(v.tensor_scalar(deg[:, :], deg[:, :], 1.0 / BIG, float(N), ALU.mult, ALU.add))
                    settle()
                    v.tensor_scalar(deg[:, :], deg[:, :], DEG_EPS, None, ALU.add).then_inc(var_ready, 1)
                if s == 7:
                    dve.wait_ge(late_loaded, 48)
                    dve.wait_ge(aux_done, 2 * job(H - 1, "max", 2 * NT - 1) + 2)
                    hi, lo = (wo_parts[:, a, :, :].rearrange("p c d -> p (c d)") for a in range(2))
                    flat = wo.rearrange("p c d -> p (c d)")
                    link(v.tensor_scalar(hi, flat, WS, None, ALU.mult))
                    settle()
                    v.scalar_tensor_tensor(out=lo, in0=flat, scalar=WS, in1=hi, op0=ALU.mult,
                                           op1=ALU.subtract).then_inc(wo_split, 1)
                if s == MP + 3:
                    dve.wait_ge(w1_tr, 1)
                    v.tensor_copy(w1T.rearrange("p a b -> p (a b)"), aux_ps[:, 1, :]).then_inc(w1_used, 1)
                for b, k in RESTORE.get(s, ()):
                    restore(b, k)

            LINKS = 3 * NB + 5
            links0 = chain["n"]

            def period(h, par, first, last):
                if not first:
                    chain["base"], chain["n"] = LINKS * h + (links0 - 3), 0
                def low(hh, st):
                    if not pool_step(st):
                        dve.wait_ge(hi_done, hh * ST + st + 1)
                        v.tensor_tensor(prob_lo(st), prob(st), prob_hi(st), ALU.subtract).then_inc(lo_dve, 1)

                def drains(slot):
                    for kind, i in at_slot[slot]:
                        if (kind, i) == CROW_LAST:
                            drain(h, kind, i, par, True)
                        elif not last:
                            drain(h + 1, kind, i, 1 - par, True)

                for s in range(ST):
                    drains(4 * s)
                    if last:
                        last_head(s)
                    if s >= 1:
                        low(h, s - 1)
                    if last and out_tile(s + 1) is not None:
                        split_heads(out_tile(s + 1), False)
                    drains(4 * s + 1)
                    drains(4 * s + 2)
                    if last and out_tile(s) is not None:
                        keep_heads_T(out_tile(s))
                    if (s - LAG) % MP == MP - 1 and s >= LAG:
                        dve.wait_ge(pv_done, h * ST + s - LAG + 1)
                        evacuate(h, (s - LAG) // MP)
                    if s == LAG - 1 and not first:
                        dve.wait_ge(pv_done, h * ST)
                        evacuate(h - 1, NB - 1)
                    if last and out_tile(s - 1) is not None:
                        if s == out_step(0) + 1:
                            dve.wait_ge(x_again, 16)
                        residual(out_tile(s - 1))
                        if out_tile(s - 1) == 2 * TB - 1:
                            variances(0, 2)
                    drains(4 * s + 3)
                low(h, ST - 1)
                if not last:
                    want = LINKS - (3 if first else 0)
                    assert chain["n"] - (links0 if first else 0) == want, (chain["n"], want)

            period(0, 0, True, False)
            with dve.Fori(0, (H - 2) // 2) as i:
                period(2 * i + 1, 1, False, False)
                period(2 * i + 2, 0, False, False)
            period(H - 1, 1, False, True)
            split_heads(IN_LOOP + 1, True)
            keep_heads_T(IN_LOOP)
            dve.wait_ge(root_ready, 3)
            newton_rsqrt(dis[:, :], deg_root[:, :], deg[:, :], newton[:, :])
            scales(0, 0, 2)
            keep_heads_T(IN_LOOP + 1)
            residual(IN_LOOP)
            dve.wait_ge(pv_done, H * ST)
            evacuate(H - 1, NB - 1)
            low_g(0)
            split_heads(NT - 4, True)
            split_heads(NT - 3, True)
            residual(IN_LOOP + 1)
            variances(2, 3)
            split_heads(NT - 2, True)
            scales(1, 2, 3)
            low_g(1)
            residual(NT - 4)
            split_heads(NT - 1, True)
            residual(NT - 3)
            residual(NT - 2)
            low_g(2)
            residual(NT - 1)
            variances(3, 4)
            scales(2, 3, 4)
            low_g(3)
            for b, k in RESTORE_LATE:
                restore(b, k)
            link(v.tensor_scalar(dis[:, :], dis[:, :], 4.0, None, ALU.mult))
            settle()
            dve.wait_ge(x2b_ready, NB)
            for t in range(NT):
                dve.wait_ge(y_done, t + 1)
                v.scalar_tensor_tensor(out=x2[:, t, :], in0=y_ps(t), scalar=dis[:, t:t + 1],
                                       in1=x2[:, t, :], op0=ALU.mult, op1=ALU.add).then_inc(y_ready, 1)

        @block.tensor
        def _(pe):
            m = nc.tensor
            pe.wait_ge(consts, NC)
            for g in range(2 * KT):
                half, t = g // KT, g % KT
                if t == 0:
                    pe.wait_ge(norm_done, half + 1)
                for u in range(8):
                    last = m.transpose(group_ps(g)[:, u * P:(u + 1) * P], h_in[:, half * 8 + u, t * P:(t + 1) * P],
                                       id32[:, :])
                last.then_inc(tr_done, 1)
            pe.wait_ge(w_split, 1)
            pe.wait_ge(tr_used, 2 * KT)

            TERMS = ((0, 0), (1, 0), (0, 1))

            def fill(h, kind, i, par, in_loop):
                n = job(h, kind, i)
                if kind == "max" and i == 0:
                    pe.wait_ge(packs_ready, 2 * h + 2)
                if kind == "crow":
                    pe.wait_ge(c_ready, NB // 2 * h + i + 1)
                def bank(c):
                    if in_loop or n >= 1:
                        pe.wait_ge(aux_done, 2 * n - 1 + c)

                if kind == "proj":
                    for c in range(2):
                        bank(c)
                        if in_loop:
                            pe.sem_inc(proj_begun, 1)
                        cols = slice(i * HALF + c * QB, i * HALF + (c + 1) * QB)
                        steps = [(t, wp, hp) for t in range(KT) for wp, hp in TERMS]
                        for k, (t, wp, hp) in enumerate(steps):
                            weights = wqk[:, wp, t, :, :].rearrange("p h c -> p (h c)")
                            last = m.matmul(aux_ps[:, c, :], weights[:, bass.ds(h * 2 * KD, 2 * KD)],
                                            hT[:, hp, t, cols], start=(k == 0), stop=(k == len(steps) - 1))
                        last.then_inc(aux_ready, 1)
                elif kind == "value":
                    if not in_loop:
                        pe.wait_ge(w_split, 2)
                    bank(1)
                    for u in range(NT):
                        steps = [(t, wp, hp) for t in range(KT) for wp, hp in TERMS]
                        for k, (t, wp, hp) in enumerate(steps):
                            last = m.matmul(aux_flat[:, u * KD:(u + 1) * KD], hT[:, hp, t, u * P:(u + 1) * P],
                                            wv[:, wp, t, bass.ds(h * KD, KD)],
                                            start=(k == 0), stop=(k == len(steps) - 1))
                    last.then_inc(aux_ready, 2)
                elif kind == "max":
                    t, half = i // 2, i % 2
                    for c in range(2):
                        k0 = half * HALF + c * QB
                        bank(c)
                        m.matmul(aux_ps[:, c, :], qA(par)[:, t * P:(t + 1) * P], kA(par)[:, k0:k0 + QB],
                                 start=True, stop=True).then_inc(aux_ready, 1)
                else:
                    bank(1)
                    for u in range(2 * TB):
                        t = i * 2 * TB + u
                        last = m.matmul(aux_flat[0:1, u * P:(u + 1) * P], c16[:, par, t:t + 1],
                                        id16[:, :], start=True, stop=True)
                    last.then_inc(aux_ready, 2)

            def transpose_mask(t):
                pe.wait_ge(mask_built, t + 1)
                if t >= 2:
                    pe.wait_ge(maskT_act, t - 1)
                    if dve_kept(t - 2):
                        pe.wait_ge(maskT_dve, dve_kept(t - 2))
                for u in range(NT):
                    last = m.transpose(sc_bf(t)[:, u * P:(u + 1) * P], mask_buf(t)[:, u * P:(u + 1) * P],
                                       idb[:, :])
                last.then_inc(maskT_filled, 1)

            for t, (kind, i) in enumerate(JOBS[0:3]):
                fill(0, kind, i, 0, False)
                transpose_mask(t)
            for t in range(3, NT + 1):
                before, after = head0_jobs(t)
                for kind, i in before:
                    fill(0, kind, i, 0, False)
                if t < NT:
                    transpose_mask(t)
                for kind, i in after:
                    fill(0, kind, i, 0, False)
            pe.wait_ge(maskT_act, NT)
            pe.wait_ge(maskT_dve, dve_kept(NT - 1))

            def scores(h, s, par, first, a):
                b, pair = s // MP, s % MP
                if s % (2 * MP) == 0 and a == 0:
                    pe.wait_ge(aux_done, 2 * job(h, "crow", b // 2) + 2)
                if a == 0 and (not first or s >= 2):
                    pe.wait_ge(exp_done, h * ST + s - 1)
                q = slice(b * QB, (b + 1) * QB)
                t = 2 * pair + a
                k = slice(t * P, (t + 1) * P)
                dst = scores_ps[s % 2][:, a, :]
                m.matmul(dst, kA(par)[:, k], qA(par)[:, q], start=True, stop=False)
                m.matmul(dst, kB(par)[0:65, k], qB(par)[0:65, q], start=False, stop=False)
                last = m.matmul(dst, mask_id[:, :], mask_T[:, t, q], start=False, stop=True)
                if a == 1:
                    last.then_inc(scores_ready, 1)

            def weigh(h, s, par, first, a):
                b, pair = s // MP, s % MP
                dve_n, pool_n = lo_count(h, s)
                if a == 0 and pool_step(s):
                    pe.wait_ge(lo_pool, pool_n)
                elif a == 0:
                    pe.wait_ge(lo_dve, dve_n)
                if pair == 0 and a == 0 and not (first and b == 0):
                    pe.wait_ge(acc_used, NB * h + b)
                t = 2 * pair + a
                for u in range(TB):
                    cols = slice(a * QB + u * P, a * QB + (u + 1) * P)
                    m.matmul(acc[:, u, 0:VW], prob_hi(s)[:, cols], values[:, par, t, :],
                             start=(t == 0 and u % 2 == 0), stop=False, skip_group_check=True)
                    last = m.matmul(acc[:, u, KD:VW], prob_lo(s)[:, cols], values[:, par, t, KD:VW],
                                    start=False, stop=(t == NT - 1), skip_group_check=True)
                if a == 1:
                    last.then_inc(pv_done, 1)

            def heads_T_kept(t):
                if t < NT - TB:
                    pe.wait_ge(ot_dve, t + 1)
                else:
                    pe.wait_ge(ot_act, t - (NT - TB) + 1)

            def transpose_w1():
                pe.wait_ge(late_loaded, 48)
                pe.wait_ge(aux_done, 2 * job(H - 1, *CROW_LAST) + 2)
                for t in range(KT):
                    for u in range(KT):
                        last = m.transpose(aux_ps[:, 1, t * D + u * P:t * D + (u + 1) * P],
                                           w1_in[:, u, t * P:(t + 1) * P], id32[:, :])
                last.then_inc(w1_tr, 1)

            def transpose_heads(t):
                if t <= IN_LOOP:
                    pe.wait_ge(o_lo_pool, t + 1)
                else:
                    pe.wait_ge(o_lo_dve, t - IN_LOOP)
                if t == 0:
                    pe.wait_ge(aux_done, 2 * job(H - 1, *CROW_LAST) + 2)
                else:
                    heads_T_kept(t - 1)
                for u in range(2 * CT):
                    last = m.transpose(ot_ps[:, u * P:(u + 1) * P], o_parts(t)[:, u * P:(u + 1) * P], id16[:, :])
                last.then_inc(ot_filled, 1)

            def project_out(t):
                heads_T_kept(t)
                if t == 0:
                    pe.wait_ge(wo_split, 1)
                    pe.wait_ge(w1_used, 1)
                else:
                    pe.wait_ge(x2_done, t)
                steps = [(c, wp, op) for c in range(CT) for wp, op in TERMS]
                for k, (c, wp, op) in enumerate(steps):
                    last = m.matmul(wo_ps, ot_sb(t)[:, op * HK + c * P:op * HK + (c + 1) * P],
                                    wo_parts[:, wp, c, :], start=(k == 0), stop=(k == len(steps) - 1))
                last.then_inc(wo_done, 1)

            def period(h, par, first, last):
                def fills(slot):
                    for kind, i in at_slot[slot]:
                        if (kind, i) == CROW_LAST:
                            fill(h, kind, i, par, True)
                        elif not last:
                            fill(h + 1, kind, i, 1 - par, True)

                for s in range(ST):
                    for a in range(2):
                        scores(h, s, par, first, a)
                        fills(4 * s + a)
                        if last and a == 1 and out_tile(s) is not None:
                            transpose_heads(out_tile(s))
                    for a in range(2):
                        if s >= LAG:
                            weigh(h, s - LAG, par, first, a)
                        elif not first:
                            weigh(h - 1, ST + s - LAG, 1 - par, False, a)
                        fills(4 * s + 2 + a)
                        if last and a == 0 and out_tile(s - 1) is not None:
                            project_out(out_tile(s - 1))
                    if last and s == MP + 1:
                        transpose_w1()

            period(0, 0, True, False)
            with pe.Fori(0, (H - 2) // 2) as i:
                period(2 * i + 1, 1, False, False)
                period(2 * i + 2, 0, False, False)
            period(H - 1, 1, False, True)
            for n, s in enumerate(range(ST - LAG, ST)):
                if n < 2:
                    transpose_heads(IN_LOOP + n)
                for a in range(2):
                    weigh(H - 1, s, 1, False, a)
                if n != 1:
                    project_out(IN_LOOP + (n + 1) // 2)
            def aggregate(b, t):
                for c in range(KT):
                    for part in range(2):
                        last = m.matmul(agg_ps(b)[:, c, :], g_split[:, t, part, c * P:(c + 1) * P],
                                        mask_T[:, t, b * QB:(b + 1) * QB],
                                        start=(t == 0 and part == 0), stop=(t == NT - 1 and part == 1))
                if t == NT - 1:
                    last.then_inc(agg_done, 1)

            def first_blocks(t):
                if t % TB == 0:
                    pe.wait_ge(g_ready, t // TB + 1)
                for b in range(2):
                    aggregate(b, t)

            def transform(b):
                pe.wait_ge(agg_ready, max(b + 1, 2))
                for u in range(TB):
                    if b * TB + u >= 4:
                        pe.wait_ge(y_ready, b * TB + u - 3)
                    for c in range(KT):
                        last = m.matmul(y_ps(b * TB + u),
                                        agg_sb(b)[:, c * QB + u * P:c * QB + (u + 1) * P],
                                        w1T[:, c, :], start=(c == 0), stop=(c == KT - 1))
                    last.then_inc(y_done, 1)

            pe.wait_ge(adjT_ready, 2 * TB)
            for n in range(4):
                first_blocks(2 * n)
                transpose_heads(NT - 4 + n)
                first_blocks(2 * n + 1)
                project_out(NT - 4 + n)
            for t in range(8, NT):
                first_blocks(t)
            for b in range(2, NB):
                pe.wait_ge(adjT_ready, (b + 1) * TB)
                if b == 2:
                    pe.wait_ge(x2_done, NT)
                for t in range(NT):
                    aggregate(b, t)
                transform(b - 2)
            transform(NB - 2)
            transform(NB - 1)


def mask_constants():
    best = None
    for i in range(1024):
        step = 1 + i / 1024
        want = 0.01 / step
        unit = 2.0 ** (-7 - 7)
        if want < 2.0 ** -7:
            unit /= 2
        eps = round(want / unit) * unit
        miss = abs(step * eps - 0.01)
        if best is None or miss < best[0]:
            best = (miss, step, eps)
    assert best[0] < 2e-8
    return best[1], best[2]


_INS = ['x', 'adj', 'L0_gnn_Wks', 'L0_gnn_Wqs', 'L0_gnn_Wvs', 'L0_gnn_Wo', 'L1_gnn_W', 'L1_gnn_b']
_OUTS = [((2048, 256), 'float32')]


def kernel(**inputs):
    import numpy as _np
    import concourse.bacc as _bacc
    from concourse import mybir as _mybir
    from concourse.bass_utils import run_bass_kernel_spmd as _run

    nc = _bacc.Bacc("TRN2", target_bir_lowering=False, num_devices=1)
    arrays, args = {}, []
    for name in _INS:
        a = _np.ascontiguousarray(inputs[name])
        arrays[f"in_{name}_dram"] = a
        args.append(nc.dram_tensor(f"in_{name}_dram", a.shape, _mybir.dt.from_np(a.dtype), kind="ExternalInput").ap())
    for i, (shape, dtype) in enumerate(_OUTS):
        dt = _mybir.dt.from_np(_np.dtype(dtype))
        args.append(nc.dram_tensor(f"out_{i}_dram", shape, dt, kind="ExternalOutput").ap())
    adj_preln_kernel(nc, *args)
    r = _run(nc, [arrays], core_ids=[0])
    got = tuple(r.results[0][f"out_{i}_dram"] for i in range(len(_OUTS)))
    return got[0]
```
